# Optimizing a Trainium2 kernel written in Bass

```python
import numpy as np
import jax
import jax.numpy as jnp

def _softmax(x, axis=-1):
    return jax.nn.softmax(x, axis=axis)
def _gelu(x):
    return jax.nn.gelu(x, approximate=True)
def _silu(x):
    return jax.nn.silu(x)
def _sigmoid(x):
    return jax.nn.sigmoid(x)
def _layernorm(x, axis=-1, eps=1e-5):
    m = jnp.mean(x, axis=axis, keepdims=True)
    v = jnp.var(x, axis=axis, keepdims=True)
    return (x - m) / jnp.sqrt(v + eps)
def _scatter_add(tgt, idx, src, axis=0):
    return tgt.at[idx].add(src)
def _segment_sum(src, seg, n):
    return jax.ops.segment_sum(src, seg, n)

kernel_name = 'mk_conv_preact_d2_conv_nchw192_451a96'

def setup_inputs(seed: int = 0):
    np.random.seed(seed)
    _w = jnp.asarray
    def _rec_inputs():
        import jax
        import jax.numpy as jnp
        _gk = jax.random.key(seed)
        x = -0.0004039 + 1 * jax.random.normal(jax.random.fold_in(_gk, 1), (4, 192, 128, 128), jnp.float32)
        return x
    x = _rec_inputs()
    def _L0_conv_setup():
        import jax, jax.numpy as jnp
        import numpy as np
        import math
        C64 = jnp.complex64

        def _fftconv_full(a, kern):
            L = a.shape[-1] + kern.shape[0] - 1
            A = jnp.fft.fft(a, n=L, axis=-1)
            K = jnp.fft.fft(kern.astype(a.dtype), n=L)
            return jnp.fft.ifft(A * K, axis=-1)

        def _centered_ifft(f):
            N = f.shape[-1]
            shft = (np.arange(N) + int(np.fix(N / 2))) % N
            inv = np.argsort(shft)
            g = jnp.fft.ifft(f[..., shft], axis=-1) * math.sqrt(N)
            return g[..., inv].astype(f.dtype)

        def _sincinterp(f):
            N = f.shape[-1]
            y = jnp.zeros(f.shape[:-1] + (2 * N - 1,), f.dtype).at[..., ::2].set(f)
            kern = jnp.asarray(np.sinc(np.arange(-(2 * N - 3), 2 * N - 2) / 2.0).astype(np.complex64))
            return _fftconv_full(y, kern)[..., 2 * N - 3:4 * N - 4]

        def _frft_chirp(f, a):
            N = f.shape[-1]
            alpha = a * math.pi / 2
            tana2, sina = (math.tan(alpha / 2), math.sin(alpha))
            fi = _sincinterp(f)
            pad = jnp.zeros(f.shape[:-1] + (N - 1,), f.dtype)
            fp = jnp.concatenate([pad, fi, pad], axis=-1)
            n = np.arange(-2 * N + 2, 2 * N - 1).astype(np.float64)
            chrp = jnp.asarray(np.exp(-1j * math.pi / N * tana2 / 4 * n ** 2).astype(np.complex64))
            fp = chrp * fp
            c = math.pi / N / sina / 4
            m = np.arange(-(4 * N - 4), 4 * N - 3).astype(np.float64)
            kern = jnp.asarray(np.exp(1j * c * m ** 2).astype(np.complex64))
            ret = _fftconv_full(fp, kern)[..., 4 * N - 4:8 * N - 7] * math.sqrt(c / math.pi)
            ret = chrp * ret
            phase = np.complex64(np.exp(-1j * (1 - a) * math.pi / 4))
            return phase * ret[..., N - 1:3 * N - 2:2]

        def _frft_last(f, a):
            if a < 0.5:
                f = _centered_ifft(f)
                a = a + 1.0
            return _frft_chirp(f, a)

        def _frft2d(x, a):
            t = _frft_last(x, a)
            return jnp.swapaxes(_frft_last(jnp.swapaxes(t, -1, -2), a), -1, -2)

        def _c1x1(x, w, b=None):
            y = jnp.einsum('nchw,oc->nohw', x, w)
            return y if b is None else y + b[None, :, None, None]

        def _c3x3(x, w, b):
            y = jax.lax.conv_general_dilated(x, w, (1, 1), 'SAME', dimension_numbers=('NCHW', 'OIHW', 'NCHW'))
            return y + b[None, :, None, None]

        def _forward(x, conv1_w, mag_s_w, mag_s_b, mag_f_w, mag_f_b, mag_w, mag_b, pha_w, pha_b, conv_0_w, conv_0_b, conv_1_w, conv_1_b, conv2_w):
            angle = 0.5
            alpha = math.cos(angle * math.pi / 2)
            N, C, H, W = x.shape
            H1, W1 = (int(H * alpha), int(W * alpha))
            x1 = _c1x1(x, conv1_w)
            C1, C0 = (C // 4, C // 4 // 3)
            x_0, x_05, x_1 = (x1[:, :C0], x1[:, C0:C1 - C0], x1[:, C1 - C0:C1])
            h0, w0 = ((H - H1) // 2, (W - W1) // 2)
            mask1 = jnp.zeros((H, W), jnp.float32).at[h0:h0 + H1, w0:w0 + W1].set(1.0)
            mask2 = 1.0 - mask1
            Fre = _frft2d(x_05.astype(C64), angle)
            mag, pha = (jnp.abs(Fre), jnp.angle(Fre))
            mag_out = _c1x1(_c3x3(mag * mask1, mag_s_w, mag_s_b) * mask1 + _c1x1(mag * mask2, mag_f_w, mag_f_b) * mask2, mag_w, mag_b)
            pha_out = _c1x1(pha, pha_w, pha_b)
            Fre_out = jax.lax.complex(mag_out * jnp.cos(pha_out), mag_out * jnp.sin(pha_out))
            ifrft = jnp.abs(_frft2d(Fre_out, -angle))
            fre = jnp.fft.rfft2(x_1)
            fm, fp = (jnp.abs(fre), jnp.angle(fre))
            mo = _c1x1(fm, conv_1_w, conv_1_b)
            po = _c1x1(fp, conv_1_w, conv_1_b)
            x_1o = jnp.fft.irfft2(jax.lax.complex(mo * jnp.cos(po), mo * jnp.sin(po)), s=(H, W))
            x_0o = _c1x1(x_0, conv_0_w, conv_0_b)
            return _c1x1(jnp.concatenate([x_0o, ifrft, x_1o], axis=1), conv2_w)
        key = jax.random.key(seed)
        ks = jax.random.split(key, 16)
        N, C, H, W, Co = (4, 192, 128, 128, 192)
        C1, C0 = (C // 4, C // 4 // 3)
        Cm = C1 - 2 * C0
        s = 0.05
        r = lambda k, sh: jax.random.normal(k, sh, jnp.float32)
        return {'x': r(ks[0], (N, C, H, W)), 'conv1_w': r(ks[1], (C1, C)) * s, 'mag_s_w': r(ks[2], (Cm, Cm, 3, 3)) * s, 'mag_s_b': r(ks[3], (Cm,)) * s, 'mag_f_w': r(ks[4], (Cm, Cm)) * s, 'mag_f_b': r(ks[5], (Cm,)) * s, 'mag_w': r(ks[6], (Cm, Cm)) * s, 'mag_b': r(ks[7], (Cm,)) * s, 'pha_w': r(ks[8], (Cm, Cm)) * s, 'pha_b': r(ks[9], (Cm,)) * s, 'conv_0_w': r(ks[10], (C0, C0)) * s, 'conv_0_b': r(ks[11], (C0,)) * s, 'conv_1_w': r(ks[12], (C0, C0)) * s, 'conv_1_b': r(ks[13], (C0,)) * s, 'conv2_w': r(ks[14], (Co, C1)) * s}
    _L0_conv_all = _L0_conv_setup()
    _L0_conv_in = {k: v for k, v in _L0_conv_all.items() if k in ('conv1_w', 'mag_s_w', 'mag_s_b', 'mag_f_w', 'mag_f_b', 'mag_w', 'mag_b', 'pha_w', 'pha_b', 'conv_0_w', 'conv_0_b', 'conv_1_w', 'conv_1_b', 'conv2_w', )}
    del _L0_conv_all

    def _L1_conv_setup():
        import jax, jax.numpy as jnp
        import numpy as np
        B, C, H, W = (4, 192, 64, 64)
        D_STATE = 16
        EXPAND = 2
        D_CONV = 4
        DI = EXPAND * C
        R = (C + 15) // 16
        K = 4

        def _dwconv(x, w, b, pad):
            y = jax.lax.conv_general_dilated(x, w, (1, 1), pad, dimension_numbers=('NCHW', 'OIHW', 'NCHW'), feature_group_count=x.shape[1])
            return y + b[None, :, None, None]

        def _forward(x, W_in, b_in, conv_w, conv_b, x_proj_w, dt_proj_w, dt_proj_b, A_log, Ds, ln_g, ln_b, W_out, b_out, dw_w, dw_b, bn_g, bn_b, bn_mean, bn_var, pw_w, pw_b, r_w, r_b):
            Bb, Cc, Hh, Ww = x.shape
            L = Hh * Ww
            silu = jax.nn.silu
            xz = jnp.einsum('bchw,cd->bdhw', x, W_in) + b_in[None, :, None, None]
            x_in, z = (xz[:, :DI], xz[:, DI:])
            xc = silu(_dwconv(x_in, conv_w, conv_b, ((1, 2), (1, 2))))
            x_hw = xc.reshape(Bb, DI, L)
            x_wh = jnp.transpose(xc, (0, 1, 3, 2)).reshape(Bb, DI, L)
            xs = jnp.stack([x_hw, x_wh, x_hw[..., ::-1], x_wh[..., ::-1]], axis=1)
            x_dbl = jnp.einsum('bkdl,krd->bkrl', xs, x_proj_w)
            dtr = x_dbl[:, :, :R]
            Bm = x_dbl[:, :, R:R + D_STATE]
            Cm = x_dbl[:, :, R + D_STATE:]
            dt = jax.nn.softplus(jnp.einsum('bkrl,kdr->bkdl', dtr, dt_proj_w) + dt_proj_b[None, :, :, None])
            A = -jnp.exp(A_log)

            def step(h, inp):
                u_t, dt_t, B_t, C_t = inp
                dA = jnp.exp(dt_t[..., None] * A[None])
                h = h * dA + (dt_t * u_t)[..., None] * B_t[:, :, None, :]
                y = jnp.sum(h * C_t[:, :, None, :], axis=-1)
                return (h, y)
            h0 = jnp.zeros((Bb, K, DI, D_STATE), x.dtype)
            seq = (jnp.moveaxis(xs, 3, 0), jnp.moveaxis(dt, 3, 0), jnp.moveaxis(Bm, 3, 0), jnp.moveaxis(Cm, 3, 0))
            _, ys = jax.lax.scan(step, h0, seq)
            ys = jnp.moveaxis(ys, 0, 3) + Ds[None, :, :, None] * xs
            inv_wh = lambda t: jnp.transpose(t.reshape(Bb, DI, Ww, Hh), (0, 1, 3, 2)).reshape(Bb, DI, L)
            y = ys[:, 0] + inv_wh(ys[:, 1]) + ys[:, 2][..., ::-1] + inv_wh(ys[:, 3][..., ::-1])
            y = jnp.transpose(y.reshape(Bb, DI, Hh, Ww), (0, 2, 3, 1))
            mu = y.mean(-1, keepdims=True)
            var = y.var(-1, keepdims=True)
            y = (y - mu) / jnp.sqrt(var + 1e-05) * ln_g + ln_b
            y = y * silu(jnp.transpose(z, (0, 2, 3, 1)))
            g_out = jnp.transpose(y @ W_out + b_out, (0, 3, 1, 2))
            l = _dwconv(x, dw_w, dw_b, ((1, 1), (1, 1)))
            l = (l - bn_mean[None, :, None, None]) / jnp.sqrt(bn_var + 1e-05)[None, :, None, None] * bn_g[None, :, None, None] + bn_b[None, :, None, None]
            l = jax.nn.relu(l)
            l_out = jnp.einsum('bchw,oc->bohw', l, pw_w) + pw_b[None, :, None, None]
            wts = jax.nn.softmax(x.mean((2, 3)) @ r_w.T + r_b, axis=1)
            return wts[:, 0, None, None, None] * g_out + wts[:, 1, None, None, None] * l_out
        key = jax.random.key(seed)
        ks = jax.random.split(key, 16)
        n = lambda i, shape, s=0.02: jax.random.normal(ks[i], shape, jnp.float32) * s
        return {'x': jax.random.normal(ks[0], (B, C, H, W), jnp.float32), 'W_in': n(1, (C, 2 * DI)), 'b_in': jnp.zeros((2 * DI,), jnp.float32), 'conv_w': n(2, (DI, 1, D_CONV, D_CONV), 0.1), 'conv_b': jnp.zeros((DI,), jnp.float32), 'x_proj_w': n(3, (K, R + 2 * D_STATE, DI)), 'dt_proj_w': n(4, (K, DI, R), 0.1), 'dt_proj_b': n(5, (K, DI), 0.5), 'A_log': jnp.tile(jnp.log(jnp.arange(1, D_STATE + 1, dtype=jnp.float32)), (K, DI, 1)), 'Ds': jnp.ones((K, DI), jnp.float32), 'ln_g': jnp.ones((DI,), jnp.float32), 'ln_b': jnp.zeros((DI,), jnp.float32), 'W_out': n(6, (DI, C)), 'b_out': jnp.zeros((C,), jnp.float32), 'dw_w': n(7, (C, 1, 3, 3), 0.1), 'dw_b': jnp.zeros((C,), jnp.float32), 'bn_g': jnp.ones((C,), jnp.float32), 'bn_b': jnp.zeros((C,), jnp.float32), 'bn_mean': jnp.zeros((C,), jnp.float32), 'bn_var': jnp.ones((C,), jnp.float32), 'pw_w': n(8, (C, C)), 'pw_b': jnp.zeros((C,), jnp.float32), 'r_w': n(9, (2, C)), 'r_b': jnp.zeros((2,), jnp.float32)}
    _L1_conv_all = _L1_conv_setup()
    _L1_conv_in = {k: v for k, v in _L1_conv_all.items() if k in ('W_in', 'b_in', 'conv_w', 'conv_b', 'x_proj_w', 'dt_proj_w', 'dt_proj_b', 'A_log', 'Ds', 'ln_g', 'ln_b', 'W_out', 'b_out', 'dw_w', 'dw_b', 'bn_g', 'bn_b', 'bn_mean', 'bn_var', 'pw_w', 'pw_b', 'r_w', 'r_b', )}
    del _L1_conv_all

    return {
        "x": x,
        "L0_conv_conv1_w": _L0_conv_in["conv1_w"],
        "L0_conv_mag_s_w": _L0_conv_in["mag_s_w"],
        "L0_conv_mag_s_b": _L0_conv_in["mag_s_b"],
        "L0_conv_mag_f_w": _L0_conv_in["mag_f_w"],
        "L0_conv_mag_f_b": _L0_conv_in["mag_f_b"],
        "L0_conv_mag_w": _L0_conv_in["mag_w"],
        "L0_conv_mag_b": _L0_conv_in["mag_b"],
        "L0_conv_pha_w": _L0_conv_in["pha_w"],
        "L0_conv_pha_b": _L0_conv_in["pha_b"],
        "L0_conv_conv_0_w": _L0_conv_in["conv_0_w"],
        "L0_conv_conv_0_b": _L0_conv_in["conv_0_b"],
        "L0_conv_conv_1_w": _L0_conv_in["conv_1_w"],
        "L0_conv_conv_1_b": _L0_conv_in["conv_1_b"],
        "L0_conv_conv2_w": _L0_conv_in["conv2_w"],
        "L1_conv_W_in": _L1_conv_in["W_in"],
        "L1_conv_b_in": _L1_conv_in["b_in"],
        "L1_conv_conv_w": _L1_conv_in["conv_w"],
        "L1_conv_conv_b": _L1_conv_in["conv_b"],
        "L1_conv_x_proj_w": _L1_conv_in["x_proj_w"],
        "L1_conv_dt_proj_w": _L1_conv_in["dt_proj_w"],
        "L1_conv_dt_proj_b": _L1_conv_in["dt_proj_b"],
        "L1_conv_A_log": _L1_conv_in["A_log"],
        "L1_conv_Ds": _L1_conv_in["Ds"],
        "L1_conv_ln_g": _L1_conv_in["ln_g"],
        "L1_conv_ln_b": _L1_conv_in["ln_b"],
        "L1_conv_W_out": _L1_conv_in["W_out"],
        "L1_conv_b_out": _L1_conv_in["b_out"],
        "L1_conv_dw_w": _L1_conv_in["dw_w"],
        "L1_conv_dw_b": _L1_conv_in["dw_b"],
        "L1_conv_bn_g": _L1_conv_in["bn_g"],
        "L1_conv_bn_b": _L1_conv_in["bn_b"],
        "L1_conv_bn_mean": _L1_conv_in["bn_mean"],
        "L1_conv_bn_var": _L1_conv_in["bn_var"],
        "L1_conv_pw_w": _L1_conv_in["pw_w"],
        "L1_conv_pw_b": _L1_conv_in["pw_b"],
        "L1_conv_r_w": _L1_conv_in["r_w"],
        "L1_conv_r_b": _L1_conv_in["r_b"],
    }

def reference(x, L0_conv_conv1_w, L0_conv_mag_s_w, L0_conv_mag_s_b, L0_conv_mag_f_w, L0_conv_mag_f_b, L0_conv_mag_w, L0_conv_mag_b, L0_conv_pha_w, L0_conv_pha_b, L0_conv_conv_0_w, L0_conv_conv_0_b, L0_conv_conv_1_w, L0_conv_conv_1_b, L0_conv_conv2_w, L1_conv_W_in, L1_conv_b_in, L1_conv_conv_w, L1_conv_conv_b, L1_conv_x_proj_w, L1_conv_dt_proj_w, L1_conv_dt_proj_b, L1_conv_A_log, L1_conv_Ds, L1_conv_ln_g, L1_conv_ln_b, L1_conv_W_out, L1_conv_b_out, L1_conv_dw_w, L1_conv_dw_b, L1_conv_bn_g, L1_conv_bn_b, L1_conv_bn_mean, L1_conv_bn_var, L1_conv_pw_w, L1_conv_pw_b, L1_conv_r_w, L1_conv_r_b):
    import jax
    import jax.numpy as jnp
    def _L0_conv_ref(x, conv1_w, mag_s_w, mag_s_b, mag_f_w, mag_f_b, mag_w, mag_b, pha_w, pha_b, conv_0_w, conv_0_b, conv_1_w, conv_1_b, conv2_w):
        import jax, jax.numpy as jnp
        import numpy as np
        import math
        C64 = jnp.complex64

        def _fftconv_full(a, kern):
            L = a.shape[-1] + kern.shape[0] - 1
            A = jnp.fft.fft(a, n=L, axis=-1)
            K = jnp.fft.fft(kern.astype(a.dtype), n=L)
            return jnp.fft.ifft(A * K, axis=-1)

        def _centered_ifft(f):
            N = f.shape[-1]
            shft = (np.arange(N) + int(np.fix(N / 2))) % N
            inv = np.argsort(shft)
            g = jnp.fft.ifft(f[..., shft], axis=-1) * math.sqrt(N)
            return g[..., inv].astype(f.dtype)

        def _sincinterp(f):
            N = f.shape[-1]
            y = jnp.zeros(f.shape[:-1] + (2 * N - 1,), f.dtype).at[..., ::2].set(f)
            kern = jnp.asarray(np.sinc(np.arange(-(2 * N - 3), 2 * N - 2) / 2.0).astype(np.complex64))
            return _fftconv_full(y, kern)[..., 2 * N - 3:4 * N - 4]

        def _frft_chirp(f, a):
            N = f.shape[-1]
            alpha = a * math.pi / 2
            tana2, sina = (math.tan(alpha / 2), math.sin(alpha))
            fi = _sincinterp(f)
            pad = jnp.zeros(f.shape[:-1] + (N - 1,), f.dtype)
            fp = jnp.concatenate([pad, fi, pad], axis=-1)
            n = np.arange(-2 * N + 2, 2 * N - 1).astype(np.float64)
            chrp = jnp.asarray(np.exp(-1j * math.pi / N * tana2 / 4 * n ** 2).astype(np.complex64))
            fp = chrp * fp
            c = math.pi / N / sina / 4
            m = np.arange(-(4 * N - 4), 4 * N - 3).astype(np.float64)
            kern = jnp.asarray(np.exp(1j * c * m ** 2).astype(np.complex64))
            ret = _fftconv_full(fp, kern)[..., 4 * N - 4:8 * N - 7] * math.sqrt(c / math.pi)
            ret = chrp * ret
            phase = np.complex64(np.exp(-1j * (1 - a) * math.pi / 4))
            return phase * ret[..., N - 1:3 * N - 2:2]

        def _frft_last(f, a):
            if a < 0.5:
                f = _centered_ifft(f)
                a = a + 1.0
            return _frft_chirp(f, a)

        def _frft2d(x, a):
            t = _frft_last(x, a)
            return jnp.swapaxes(_frft_last(jnp.swapaxes(t, -1, -2), a), -1, -2)

        def _c1x1(x, w, b=None):
            y = jnp.einsum('nchw,oc->nohw', x, w)
            return y if b is None else y + b[None, :, None, None]

        def _c3x3(x, w, b):
            y = jax.lax.conv_general_dilated(x, w, (1, 1), 'SAME', dimension_numbers=('NCHW', 'OIHW', 'NCHW'))
            return y + b[None, :, None, None]

        def _forward(x, conv1_w, mag_s_w, mag_s_b, mag_f_w, mag_f_b, mag_w, mag_b, pha_w, pha_b, conv_0_w, conv_0_b, conv_1_w, conv_1_b, conv2_w):
            angle = 0.5
            alpha = math.cos(angle * math.pi / 2)
            N, C, H, W = x.shape
            H1, W1 = (int(H * alpha), int(W * alpha))
            x1 = _c1x1(x, conv1_w)
            C1, C0 = (C // 4, C // 4 // 3)
            x_0, x_05, x_1 = (x1[:, :C0], x1[:, C0:C1 - C0], x1[:, C1 - C0:C1])
            h0, w0 = ((H - H1) // 2, (W - W1) // 2)
            mask1 = jnp.zeros((H, W), jnp.float32).at[h0:h0 + H1, w0:w0 + W1].set(1.0)
            mask2 = 1.0 - mask1
            Fre = _frft2d(x_05.astype(C64), angle)
            mag, pha = (jnp.abs(Fre), jnp.angle(Fre))
            mag_out = _c1x1(_c3x3(mag * mask1, mag_s_w, mag_s_b) * mask1 + _c1x1(mag * mask2, mag_f_w, mag_f_b) * mask2, mag_w, mag_b)
            pha_out = _c1x1(pha, pha_w, pha_b)
            Fre_out = jax.lax.complex(mag_out * jnp.cos(pha_out), mag_out * jnp.sin(pha_out))
            ifrft = jnp.abs(_frft2d(Fre_out, -angle))
            fre = jnp.fft.rfft2(x_1)
            fm, fp = (jnp.abs(fre), jnp.angle(fre))
            mo = _c1x1(fm, conv_1_w, conv_1_b)
            po = _c1x1(fp, conv_1_w, conv_1_b)
            x_1o = jnp.fft.irfft2(jax.lax.complex(mo * jnp.cos(po), mo * jnp.sin(po)), s=(H, W))
            x_0o = _c1x1(x_0, conv_0_w, conv_0_b)
            return _c1x1(jnp.concatenate([x_0o, ifrft, x_1o], axis=1), conv2_w)
        return _forward(x, conv1_w, mag_s_w, mag_s_b, mag_f_w, mag_f_b, mag_w, mag_b, pha_w, pha_b, conv_0_w, conv_0_b, conv_1_w, conv_1_b, conv2_w)

    def _L1_conv_ref(x, W_in, b_in, conv_w, conv_b, x_proj_w, dt_proj_w, dt_proj_b, A_log, Ds, ln_g, ln_b, W_out, b_out, dw_w, dw_b, bn_g, bn_b, bn_mean, bn_var, pw_w, pw_b, r_w, r_b):
        import jax, jax.numpy as jnp
        import numpy as np
        B, C, H, W = (4, 192, 64, 64)
        D_STATE = 16
        EXPAND = 2
        D_CONV = 4
        DI = EXPAND * C
        R = (C + 15) // 16
        K = 4

        def _dwconv(x, w, b, pad):
            y = jax.lax.conv_general_dilated(x, w, (1, 1), pad, dimension_numbers=('NCHW', 'OIHW', 'NCHW'), feature_group_count=x.shape[1])
            return y + b[None, :, None, None]

        def _forward(x, W_in, b_in, conv_w, conv_b, x_proj_w, dt_proj_w, dt_proj_b, A_log, Ds, ln_g, ln_b, W_out, b_out, dw_w, dw_b, bn_g, bn_b, bn_mean, bn_var, pw_w, pw_b, r_w, r_b):
            Bb, Cc, Hh, Ww = x.shape
            L = Hh * Ww
            silu = jax.nn.silu
            xz = jnp.einsum('bchw,cd->bdhw', x, W_in) + b_in[None, :, None, None]
            x_in, z = (xz[:, :DI], xz[:, DI:])
            xc = silu(_dwconv(x_in, conv_w, conv_b, ((1, 2), (1, 2))))
            x_hw = xc.reshape(Bb, DI, L)
            x_wh = jnp.transpose(xc, (0, 1, 3, 2)).reshape(Bb, DI, L)
            xs = jnp.stack([x_hw, x_wh, x_hw[..., ::-1], x_wh[..., ::-1]], axis=1)
            x_dbl = jnp.einsum('bkdl,krd->bkrl', xs, x_proj_w)
            dtr = x_dbl[:, :, :R]
            Bm = x_dbl[:, :, R:R + D_STATE]
            Cm = x_dbl[:, :, R + D_STATE:]
            dt = jax.nn.softplus(jnp.einsum('bkrl,kdr->bkdl', dtr, dt_proj_w) + dt_proj_b[None, :, :, None])
            A = -jnp.exp(A_log)

            def step(h, inp):
                u_t, dt_t, B_t, C_t = inp
                dA = jnp.exp(dt_t[..., None] * A[None])
                h = h * dA + (dt_t * u_t)[..., None] * B_t[:, :, None, :]
                y = jnp.sum(h * C_t[:, :, None, :], axis=-1)
                return (h, y)
            h0 = jnp.zeros((Bb, K, DI, D_STATE), x.dtype)
            seq = (jnp.moveaxis(xs, 3, 0), jnp.moveaxis(dt, 3, 0), jnp.moveaxis(Bm, 3, 0), jnp.moveaxis(Cm, 3, 0))
            _, ys = jax.lax.scan(step, h0, seq)
            ys = jnp.moveaxis(ys, 0, 3) + Ds[None, :, :, None] * xs
            inv_wh = lambda t: jnp.transpose(t.reshape(Bb, DI, Ww, Hh), (0, 1, 3, 2)).reshape(Bb, DI, L)
            y = ys[:, 0] + inv_wh(ys[:, 1]) + ys[:, 2][..., ::-1] + inv_wh(ys[:, 3][..., ::-1])
            y = jnp.transpose(y.reshape(Bb, DI, Hh, Ww), (0, 2, 3, 1))
            mu = y.mean(-1, keepdims=True)
            var = y.var(-1, keepdims=True)
            y = (y - mu) / jnp.sqrt(var + 1e-05) * ln_g + ln_b
            y = y * silu(jnp.transpose(z, (0, 2, 3, 1)))
            g_out = jnp.transpose(y @ W_out + b_out, (0, 3, 1, 2))
            l = _dwconv(x, dw_w, dw_b, ((1, 1), (1, 1)))
            l = (l - bn_mean[None, :, None, None]) / jnp.sqrt(bn_var + 1e-05)[None, :, None, None] * bn_g[None, :, None, None] + bn_b[None, :, None, None]
            l = jax.nn.relu(l)
            l_out = jnp.einsum('bchw,oc->bohw', l, pw_w) + pw_b[None, :, None, None]
            wts = jax.nn.softmax(x.mean((2, 3)) @ r_w.T + r_b, axis=1)
            return wts[:, 0, None, None, None] * g_out + wts[:, 1, None, None, None] * l_out
        return _forward(x, W_in, b_in, conv_w, conv_b, x_proj_w, dt_proj_w, dt_proj_b, A_log, Ds, ln_g, ln_b, W_out, b_out, dw_w, dw_b, bn_g, bn_b, bn_mean, bn_var, pw_w, pw_b, r_w, r_b)

    def _gn(v, G=32, eps=1e-5):
        B_, C_, H_, W_ = v.shape
        g = v.reshape(B_, G, C_ // G, H_, W_)
        m = jnp.mean(g, axis=(2, 3, 4), keepdims=True)
        s = jnp.var(g, axis=(2, 3, 4), keepdims=True)
        return ((g - m) / jnp.sqrt(s + eps)).reshape(v.shape)

    def _ln_c(v, eps=1e-6):
        m = jnp.mean(v, axis=1, keepdims=True)
        s = jnp.var(v, axis=1, keepdims=True)
        return (v - m) / jnp.sqrt(s + eps)

    def _ln_t(v, eps=1e-5):
        m = jnp.mean(v, axis=-1, keepdims=True)
        s = jnp.var(v, axis=-1, keepdims=True)
        return (v - m) / jnp.sqrt(s + eps)

    def _to_tokens(v):
        B_, C_, H_, W_ = v.shape
        return v.reshape(B_, C_, H_ * W_).transpose(0, 2, 1)
    def _from_tokens(t, like):
        B_, C_, H_, W_ = like.shape
        return t.transpose(0, 2, 1).reshape(B_, C_, H_, W_)

    x = x + _L0_conv_ref(_gn(x), L0_conv_conv1_w, L0_conv_mag_s_w, L0_conv_mag_s_b, L0_conv_mag_f_w, L0_conv_mag_f_b, L0_conv_mag_w, L0_conv_mag_b, L0_conv_pha_w, L0_conv_pha_b, L0_conv_conv_0_w, L0_conv_conv_0_b, L0_conv_conv_1_w, L0_conv_conv_1_b, L0_conv_conv2_w)
    x = x + _L1_conv_ref(_gn(x), L1_conv_W_in, L1_conv_b_in, L1_conv_conv_w, L1_conv_conv_b, L1_conv_x_proj_w, L1_conv_dt_proj_w, L1_conv_dt_proj_b, L1_conv_A_log, L1_conv_Ds, L1_conv_ln_g, L1_conv_ln_b, L1_conv_W_out, L1_conv_b_out, L1_conv_dw_w, L1_conv_dw_b, L1_conv_bn_g, L1_conv_bn_b, L1_conv_bn_mean, L1_conv_bn_var, L1_conv_pw_w, L1_conv_pw_b, L1_conv_r_w, L1_conv_r_b)
    return x


_drawn_inputs = setup_inputs


def setup_inputs(seed=0):
    import zlib

    import numpy as np

    out = dict(_drawn_inputs(seed))
    spreads = {'L1_conv_b_in': (0.0, 0.64),
     'L1_conv_conv_b': (0.0, 0.381),
     'L1_conv_Ds': (1.0, 0.6),
     'L1_conv_ln_g': (1.0, 0.6),
     'L1_conv_ln_b': (0.0, 0.8),
     'L1_conv_b_out': (0.0, 0.1),
     'L1_conv_dw_b': (0.0, 0.8),
     'L1_conv_bn_g': (1.0, 0.6),
     'L1_conv_bn_b': (0.0, 0.8),
     'L1_conv_bn_mean': (0.0, 0.8),
     'L1_conv_bn_var': (1.0, 0.6),
     'L1_conv_pw_b': (0.0, 0.294),
     'L1_conv_r_b': (0.0, 0.8)}
    factors = {'L0_conv_mag_s_w': 6.976,
     'L0_conv_mag_s_b': 8.0,
     'L0_conv_mag_f_w': 8.0,
     'L0_conv_mag_f_b': 8.0,
     'L0_conv_mag_w': 7.304,
     'L0_conv_mag_b': 8.0,
     'L0_conv_pha_w': 8.0,
     'L0_conv_pha_b': 64.0,
     'L0_conv_conv_0_b': 4.611,
     'L0_conv_conv_1_b': 64.0,
     'L1_conv_x_proj_w': 8.0,
     'L1_conv_dt_proj_w': 8.0,
     'L1_conv_dt_proj_b': 8.0,
     'L1_conv_A_log': 64.0,
     'L1_conv_r_w': 8.0,
     'L1_conv_dw_w': 2.857}
    for name, (base, spread) in spreads.items():
        noise = np.random.default_rng([zlib.crc32(name.encode()), seed]).standard_normal(out[name].shape)
        drawn = base * np.exp(spread * noise) if base else spread * noise
        out[name] = jnp.asarray(drawn.astype(out[name].dtype))
    for name, factor in factors.items():
        out[name] = (out[name] * factor).astype(out[name].dtype)
    return out
```

```python
import math
from contextlib import ExitStack

import concourse.bass as bass
import numpy as np
from concourse import mybir

ALU = mybir.AluOpType
ACT = mybir.ActivationFunctionType
F32 = mybir.dt.float32
BF16 = mybir.dt.bfloat16

BATCH, CH, SIDE = 4, 192, 128
HW = SIDE * SIDE
CP = 96
CT = CH // CP
GROUP = CH // 32
MID = CH // 4
CB = MID // 3
IMAGES = CB * BATCH
HALF = SIDE // 2 + 1
INNER = int(SIDE * math.cos(0.25 * math.pi))
EDGE = (SIDE - INNER) // 2
DI = 2 * CH
NJ = DI // 128
NSTATE = 16
DT_RANK = 12
T = 512
CHUNKS = HW // T
SEQ = BATCH * CHUNKS
SLOTS = SEQ + 2
ROWS = T // SIDE
TAPS = 4
PLANE = SIDE + TAPS - 1
C_ROWS = 3 * 2 * NSTATE
SAFE_GAP = 2.0e-7
BIG = 40.0
LOG_CAP = 80.0
EPS = 1e-5


class Scope:

    def __init__(self, nc, ctx, tag):
        self.nc, self.ctx, self.tag = nc, ctx, tag
        self.sems = []
        ctx.callback(self.clear)

    def sb(self, name, shape, dtype=F32):
        return self.ctx.enter_context(self.nc.sbuf_tensor(f"{name}_{self.tag}", shape, dtype))

    def ps(self, name, shape):
        return self.ctx.enter_context(self.nc.psum_tensor(f"{name}_{self.tag}", shape, F32))

    def sem(self, name):
        self.sems.append(self.nc.alloc_semaphore(f"{name}_{self.tag}"))
        return self.sems[-1]

    def clear(self):
        self.nc.clear_and_free_semaphores(self.sems)
        self.nc.all_engine_barrier()


def row(ap, index):
    one = ap[bass.ds(index, 1)]
    names = " ".join(f"d{i}" for i in range(1, len(one.shape)))
    return one.rearrange(f"o {names} -> (o d1) {names[3:]}" if len(one.shape) > 2 else "o d1 -> o d1")


def channel_stats(nc, tag, x, stats):
    with ExitStack() as ctx:
        s = Scope(nc, ctx, tag)
        PARTS, F = 4, HW // 4
        xb = s.sb("xb", [CP, 2, F])
        st = s.sb("st", [CP, HW // T, 6])
        agg = s.sb("agg", [CP, 2])
        gate = s.sb("gate", [CP, 1])
        loaded = [s.sem("loaded0"), s.sem("loaded1")]
        counted, merged, stored, gated = s.sem("counted"), s.sem("merged"), s.sem("stored"), s.sem("gated")
        per_part = F // T
        x_v = x.rearrange("b (t c) (k f) -> (b t) c k f", c=CP, k=PARTS)
        block = ctx.enter_context(nc.Block())

        @block.sync
        def _(sp):
            with sp.Fori(0, BATCH * CT) as i:
                for k in range(PARTS):
                    sp.wait_ge(counted, i * (PARTS * per_part) + (k + 1) * per_part)
                    sp.dma_start(xb[:, k % 2, :], row(x_v, i)[:, k, :]).then_inc(loaded[k % 2], 16)

        @block.vector
        def _(dve):
            dve.sem_inc(counted, 2 * per_part)
            dve.sem_inc(gated, 1)
            with dve.Fori(0, BATCH * CT) as i:
                for k in range(PARTS):
                    dve.wait_ge(loaded[k % 2], i * (16 * PARTS // 2) + 16 * (k // 2 + 1))
                    for q in range(per_part):
                        if k == 0 and q == 0:
                            dve.wait_ge(gated, i + 1)
                            dve.wait_ge(merged, i + 1)
                        nc.vector.bn_stats(st[:, k * per_part + q, :], xb[:, k % 2, q * T:(q + 1) * T]).then_inc(counted, 1)
                dve.wait_ge(counted, i * (PARTS * per_part) + (PARTS + 2) * per_part)
                dve.wait_ge(stored, i * 16 + 16)
                nc.vector.memset(gate[:, :], 0.0).then_inc(gated, 1)
                nc.vector.bn_aggr(agg[:, :], st[:, :, :]).then_inc(merged, 1)

        @block.scalar
        def _(act):
            act.sem_inc(stored, 16)
            act.sem_inc(merged, 1)
            with act.Fori(0, BATCH * CT) as i:
                act.wait_ge(merged, i + 2)
                act.dma_start(row(stats, i), agg[:, :]).then_inc(stored, 16)
            act.wait_ge(stored, 16 * (BATCH * CT + 1))


def norm_coefficients(nc, tag, stats, group_mean, scale, shift, mean_of):
    N = BATCH * CT
    with ExitStack() as ctx:
        s = Scope(nc, ctx, tag)
        g = s.sb("g", [CP, CP])
        mv = s.sb("mv", [CP, N, 2])
        moments = s.sb("moments", [CP, 2 * N])
        grp = s.sb("grp", [CP, 2 * N])
        var = s.sb("var", [CP, N])
        std = s.sb("std", [CP, N])
        eps = s.sb("eps", [CP, 1])
        g_ps = s.ps("g_ps", [CP, 2 * N])
        loaded, chain, summed, rooted = s.sem("loaded"), s.sem("chain"), s.sem("summed"), s.sem("rooted")
        block = ctx.enter_context(nc.Block())

        @block.sync
        def _(sp):
            sp.dma_start(g[:, :], group_mean).then_inc(loaded, 16)
            sp.dma_start(mv[:, :, :], stats.rearrange("a c f -> c a f")).then_inc(loaded, 16)

        @block.tensor
        def _(pe):
            pe.wait_ge(chain, 4)
            nc.tensor.matmul(g_ps[:, :], g[:, :], moments[:, :], start=True, stop=True).then_inc(summed, 1)

        @block.scalar
        def _(act):
            act.wait_ge(chain, 7)
            nc.scalar.activation(std[:, :], var[:, :], ACT.Sqrt, bias=eps[:, 0:1]).then_inc(rooted, 1)

        @block.vector
        def _(dve):
            done = [0]

            def link(ins):
                done[0] += 1
                ins.then_inc(chain, 1)
                dve.wait_ge(chain, done[0])

            dve.wait_ge(loaded, 32)
            link(nc.vector.memset(eps[:, :], EPS))
            link(nc.vector.tensor_copy(moments[:, 0:N], mv[:, :, 0]))
            link(nc.vector.tensor_tensor(moments[:, N:2 * N], mv[:, :, 0], mv[:, :, 0], ALU.mult))
            link(nc.vector.tensor_tensor(moments[:, N:2 * N], moments[:, N:2 * N], mv[:, :, 1], ALU.add))
            dve.wait_ge(summed, 1)
            link(nc.vector.tensor_copy(grp[:, :], g_ps[:, :]))
            link(nc.vector.tensor_tensor(var[:, :], grp[:, 0:N], grp[:, 0:N], ALU.mult))
            link(nc.vector.tensor_tensor(var[:, :], grp[:, N:2 * N], var[:, :], ALU.subtract))
            dve.wait_ge(rooted, 1)
            link(nc.vector.reciprocal(scale[:, :], std[:, :]))
            link(nc.vector.scalar_tensor_tensor(out=shift[:, :], in0=grp[:, 0:N], scalar=-1.0, in1=scale[:, :], op0=ALU.mult, op1=ALU.mult))
            link(nc.vector.tensor_tensor(mean_of[:, :], moments[:, 0:N], scale[:, :], ALU.mult))
            link(nc.vector.tensor_tensor(mean_of[:, :], mean_of[:, :], shift[:, :], ALU.add))


def conv_in(nc, x, w1t, scale, shift, x1):
    F = 2 * T
    with ExitStack() as ctx:
        s = Scope(nc, ctx, "ci")
        w = s.sb("w", [CP, CT, MID])
        wb = s.sb("wb", [CP, BATCH, CT, MID])
        bias = s.sb("bias", [MID, BATCH])
        xb = s.sb("xb", [CP, 2, CT, F])
        ob = s.sb("ob", [MID, 2, F])
        o_ps = s.ps("o_ps", [MID, 2, F])
        b_ps = s.ps("b_ps", [MID, BATCH])
        w_in, w_ready, b_ready, b_kept = s.sem("w_in"), s.sem("w_ready"), s.sem("b_ready"), s.sem("b_kept")
        loaded, stored = [s.sem("loaded0"), s.sem("loaded1")], [s.sem("stored0"), s.sem("stored1")]
        multiplied, evacuated = s.sem("multiplied"), s.sem("evacuated")
        steps = HW // F // 2
        x_v = x.rearrange("b (t c) (k f) -> b k c t f", c=CP, f=F)
        o_v = x1.rearrange("o b (k f) -> b k o f", f=F)
        shift_v = shift[:, :].rearrange("c (b t) -> c t b", t=CT)
        block = ctx.enter_context(nc.Block())

        @block.sync
        def _(sp):
            sp.dma_start(w[:, :, :], w1t.rearrange("(t c) o -> c t o", c=CP)).then_inc(w_in, 16)
            for b in range(BATCH):
                with sp.Fori(0, steps) as i:
                    for u in range(2):
                        sp.wait_ge(multiplied, (b * steps + i) * 2 + u + 1)
                        sp.dma_start(xb[:, u], row(x_v[b], i * 2 + u)).then_inc(loaded[u], 16)

        @block.vector
        def _(dve):
            dve.wait_ge(w_in, 16)
            for b in range(BATCH):
                for t in range(CT):
                    n = b * CT + t
                    nc.vector.tensor_scalar(wb[:, b, t, :], w[:, t, :], scale[:, n:n + 1], None, ALU.mult).then_inc(w_ready, 1)
            dve.wait_ge(b_ready, 1)
            nc.vector.tensor_copy(bias[:, :], b_ps[:, :]).then_inc(b_kept, 1)

        @block.tensor
        def _(pe):
            pe.sem_inc(multiplied, 2)
            pe.wait_ge(w_in, 16)
            for t in range(CT):
                last = nc.tensor.matmul(b_ps[:, :], w[:, t, :], shift_v[:, t, :], start=t == 0, stop=t == CT - 1)
            last.then_inc(b_ready, 1)
            pe.wait_ge(w_ready, BATCH * CT)
            for b in range(BATCH):
                with pe.Fori(0, steps) as i:
                    for u in range(2):
                        pe.wait_ge(loaded[u], (b * steps + i) * 16 + 16)
                        pe.wait_ge(evacuated, (b * steps + i) * 2 + u + 1)
                        for half in range(2):
                            for t in range(CT):
                                cols = slice(half * T, (half + 1) * T)
                                last = nc.tensor.matmul(o_ps[:, u, cols], wb[:, b, t, :], xb[:, u, t, cols], start=t == 0, stop=t == CT - 1)
                        last.then_inc(multiplied, 1)

        @block.scalar
        def _(act):
            act.sem_inc(evacuated, 2)
            for u in range(2):
                act.sem_inc(stored[u], 16)
            act.wait_ge(b_kept, 1)
            for b in range(BATCH):
                with act.Fori(0, steps) as i:
                    for u in range(2):
                        n = (b * steps + i) * 2 + u
                        act.wait_ge(multiplied, n + 3)
                        act.wait_ge(stored[u], (b * steps + i) * 16 + 16)
                        nc.scalar.activation(ob[:, u, :], o_ps[:, u, :], ACT.Identity, bias=bias[:, b:b + 1]).then_inc(evacuated, 1)
                        act.wait_ge(evacuated, n + 3)
                        act.dma_start(row(o_v[b], i * 2 + u), ob[:, u, :]).then_inc(stored[u], 16)
            for u in range(2):
                act.wait_ge(stored[u], 16 * (BATCH * steps + 1))


def transform(nc, tag, sources, n_in, tables, first, second, n_out, finish, results):
    G = 4
    n_src = len(sources)
    steps = IMAGES // G // 2
    width = first[0].stop - first[0].start
    cols2 = second[0].stop - second[0].start
    with ExitStack() as ctx:
        s = Scope(nc, ctx, tag)
        tab = s.sb("tab", [128, tables.shape[1]])
        xb = s.sb("xb", [128, 2, n_src, G, n_in])
        mid = s.sb("mid", [n_in, 2, G, width])
        res = s.sb("res", [128, 2, G, cols2])
        tmp = {n: s.sb(n, [128, G, n_out]) for n in ("ax", "ay", "hi", "lo", "at", "pick", "move", "sq")} if finish != "real" else {}
        mag = s.sb("mag", [128, 2, G, n_out]) if finish != "real" else None
        ang = s.sb("ang", [128, 2, G, n_out]) if finish == "polar" else None
        outs = {"polar": [mag, ang], "abs": [mag], "real": [res]}[finish]
        p1 = s.ps("p1", [n_in, 2, G, 256])
        p2 = s.ps("p2", [128, 2, G, 256])
        tab_in, loaded, stored = s.sem("tab_in"), [s.sem("loaded0"), s.sem("loaded1")], [s.sem("stored0"), s.sem("stored1")]
        first_done, mid_kept, second_done, res_kept = (s.sem(n) for n in ("first_done", "mid_kept", "second_done", "res_kept"))
        finished, chain, rooted, arcs = (s.sem(n) for n in ("finished", "chain", "rooted", "arcs"))
        LINKS = {"polar": 19, "abs": 2, "real": 0}[finish]
        views = [x.rearrange("(k g) p w -> k p g w", g=G) for x in sources]
        out_views = [x.rearrange("(k g) p w -> k p g w", g=G) for x in results]
        block = ctx.enter_context(nc.Block())

        @block.sync
        def _(sp):
            sp.dma_start(tab[:, :], tables).then_inc(tab_in, 16)
            for u in range(2):
                sp.sem_inc(stored[u], 16 * len(outs))
            if finish != "real":
                sp.sem_inc(rooted, 2)

            def load(n, u):
                sp.wait_ge(first_done, n + 1)
                for k in range(n_src):
                    sp.dma_start(xb[:, u, k], row(views[k], n)).then_inc(loaded[u], 16)

            def store(n, u):
                if finish == "real":
                    sp.wait_ge(res_kept, n + 3)
                else:
                    sp.wait_ge(finished, n + 3)
                    sp.wait_ge(rooted, n + 3)
                for o, v in zip(outs, out_views):
                    sp.dma_start(row(v, n), o[:, u]).then_inc(stored[u], 16)

            for u in range(2):
                load(u, u)
            with sp.Fori(0, steps - 1) as i:
                for u in range(2):
                    store(i * 2 + u, u)
                    load(i * 2 + u + 2, u)
            for u in range(2):
                store(2 * steps - 2 + u, u)
            for u in range(2):
                sp.wait_ge(stored[u], 16 * len(outs) * (steps + 1))

        @block.tensor
        def _(pe):
            pe.sem_inc(first_done, 2)
            pe.sem_inc(second_done, 2)
            pe.wait_ge(tab_in, 16)
            with pe.Fori(0, steps) as i:
                for u in range(2):
                    n = i * 2 + u
                    pe.wait_ge(loaded[u], i * (16 * n_src) + 16 * n_src)
                    pe.wait_ge(mid_kept, n + 1)
                    for g in range(G):
                        for k in range(n_src):
                            last = nc.tensor.matmul(p1[:, u, g, 0:width], xb[:, u, k, g, :], tab[:, first[k]], start=k == 0, stop=k == n_src - 1)
                    last.then_inc(first_done, 1)
                    pe.wait_ge(mid_kept, n + 3)
                    pe.wait_ge(res_kept, n + 1)
                    for g in range(G):
                        for k in range(2):
                            last = nc.tensor.matmul(p2[:, u, g, 0:cols2], mid[:, u, g, k * 128:(k + 1) * 128], tab[0:n_in, second[k]], start=k == 0, stop=k == 1)
                    last.then_inc(second_done, 1)

        @block.scalar
        def _(act):
            act.sem_inc(mid_kept, 2)
            act.sem_inc(res_kept, 2)
            with act.Fori(0, steps) as i:
                for u in range(2):
                    n = i * 2 + u
                    act.wait_ge(first_done, n + 3)
                    act.wait_ge(second_done, n + 1)
                    nc.scalar.copy(mid[:, u], p1[:, u, :, 0:width]).then_inc(mid_kept, 1)
                    act.wait_ge(second_done, n + 3)
                    if finish == "real":
                        act.wait_ge(stored[u], i * 16 + 16)
                    else:
                        act.wait_ge(finished, n + 1)
                    nc.scalar.copy(res[:, u], p2[:, u, :, 0:cols2]).then_inc(res_kept, 1)
                    if finish != "real":
                        if finish == "abs":
                            act.wait_ge(finished, n + 3)
                        else:
                            act.wait_ge(chain, n * LINKS + 3)
                        act.wait_ge(stored[u], i * (16 * len(outs)) + 16 * len(outs))
                        nc.scalar.activation(mag[:, u], tmp["sq"][:, :, :], ACT.Sqrt).then_inc(rooted, 1)
                    if finish == "polar":
                        act.wait_ge(chain, n * LINKS + 10)
                        nc.scalar.activation(tmp["at"][:, :, :], tmp["lo"][:, :, :], ACT.Arctan).then_inc(arcs, 1)

        @block.vector
        def _(dve):
            if finish == "real":
                return
            dve.sem_inc(finished, 2)
            with dve.Fori(0, steps) as i:
                for u in range(2):
                    n = i * 2 + u
                    done = [0]

                    def link(ins):
                        done[0] += 1
                        ins.then_inc(chain, 1)
                        dve.wait_ge(chain, n * LINKS + done[0])

                    re, im = res[:, u, :, 0:n_out], res[:, u, :, n_out:2 * n_out]
                    ax, ay, hi, lo, at, pick, move, sq = ([tmp[k][:, :, :] for k in ("ax", "ay", "hi", "lo", "at", "pick", "move", "sq")])
                    dve.wait_ge(res_kept, n + 3)
                    dve.wait_ge(finished, n + 2)
                    dve.wait_ge(rooted, n + 2)
                    link(nc.vector.tensor_tensor(ax, re, re, ALU.mult))
                    link(nc.vector.tensor_tensor(ay, im, im, ALU.mult))
                    if finish == "abs":
                        nc.vector.tensor_tensor(sq, ax, ay, ALU.add).then_inc(finished, 1)
                        continue
                    link(nc.vector.tensor_tensor(sq, ax, ay, ALU.add))
                    link(nc.vector.scalar_tensor_tensor(out=ax, in0=re, scalar=-1.0, in1=re, op0=ALU.mult, op1=ALU.max))
                    link(nc.vector.scalar_tensor_tensor(out=ay, in0=im, scalar=-1.0, in1=im, op0=ALU.mult, op1=ALU.max))
                    link(nc.vector.tensor_tensor(hi, ax, ay, ALU.max))
                    link(nc.vector.tensor_scalar(hi, hi, 1e-30, None, ALU.max))
                    link(nc.vector.reciprocal(hi, hi))
                    link(nc.vector.tensor_tensor(lo, ax, ay, ALU.min))
                    link(nc.vector.tensor_tensor(lo, lo, hi, ALU.mult))
                    link(nc.vector.tensor_tensor(pick, ay, ax, ALU.is_gt))
                    dve.wait_ge(arcs, n + 1)
                    link(nc.vector.tensor_scalar(move, at, -2.0, math.pi / 2, ALU.mult, ALU.add))
                    link(nc.vector.tensor_tensor(move, move, pick, ALU.mult))
                    link(nc.vector.tensor_tensor(ax, at, move, ALU.add))
                    link(nc.vector.tensor_scalar(pick, re, 0.0, None, ALU.is_lt))
                    link(nc.vector.tensor_scalar(move, ax, -2.0, math.pi, ALU.mult, ALU.add))
                    link(nc.vector.tensor_tensor(move, move, pick, ALU.mult))
                    link(nc.vector.tensor_tensor(ax, ax, move, ALU.add))
                    link(nc.vector.tensor_scalar(pick, im, 0.0, -2.0, ALU.is_lt, ALU.mult))
                    dve.wait_ge(stored[u], i * 32 + 32)
                    nc.vector.scalar_tensor_tensor(out=ang[:, u], in0=pick, scalar=1.0, in1=ax, op0=ALU.add, op1=ALU.mult).then_inc(finished, 1)


def load_kron(eng, tile, weight_t, sem):
    for b in range(BATCH):
        eng.dma_start(tile[b:IMAGES:BATCH, b:IMAGES:BATCH], weight_t, allow_slow_non_contiguous=True).then_inc(sem, 16)


def inner_mix(nc, mag, conv_w, conv_b, flat_w, flat_b, mixed):
    WIN = INNER + 2
    BAND = 5
    assert INNER % BAND == 0
    bands = INNER // BAND
    with ExitStack() as ctx:
        s = Scope(nc, ctx, "im")
        whole = s.sb("whole", [IMAGES, SIDE, SIDE])
        window = s.sb("window", [IMAGES, WIN, WIN])
        out = s.sb("out", [IMAGES, SIDE, SIDE])
        taps = s.sb("taps", [IMAGES, 9, IMAGES])
        flat = s.sb("flat", [IMAGES, IMAGES])
        bias = s.sb("bias", [IMAGES, 2])
        p = s.ps("p", [IMAGES, 4, T])
        zeroed, w_in, loaded, cut, product, kept, stored = (s.sem(n) for n in ("zeroed", "w_in", "loaded", "cut", "product", "kept", "stored"))
        total = CHUNKS + bands
        block = ctx.enter_context(nc.Block())

        @block.sync
        def _(sp):
            sp.dma_start(whole[:, :, :], mag.rearrange("i (h w) -> i h w", h=SIDE)).then_inc(loaded, 16)
            for k, b_dram in enumerate((flat_b, conv_b)):
                sp.dma_start(bias[:, k:k + 1], b_dram).then_inc(w_in, 16)
            sp.wait_ge(zeroed, 3)
            load_kron(sp, flat, flat_w, w_in)
            for k in range(9):
                load_kron(sp, taps[:, k, :], conv_w[k], w_in)
            sp.wait_ge(kept, total + 4)
            sp.dma_start(mixed.rearrange("i (h w) -> i h w", h=SIDE), out[:, :, :]).then_inc(stored, 16)
            sp.wait_ge(stored, 16)

        @block.vector
        def _(dve):
            nc.vector.memset(flat[:, :], 0.0).then_inc(zeroed, 1)
            nc.vector.memset(taps[:, :, :], 0.0).then_inc(zeroed, 1)
            nc.vector.memset(window[:, :, :], 0.0).then_inc(zeroed, 1)
            dve.wait_ge(zeroed, 3)
            dve.wait_ge(loaded, 16)
            nc.vector.tensor_copy(window[:, 1:1 + INNER, 1:1 + INNER], whole[:, EDGE:EDGE + INNER, EDGE:EDGE + INNER]).then_inc(cut, 1)

        @block.tensor
        def _(pe):
            pe.wait_ge(loaded, 16)
            pe.wait_ge(w_in, 16 * (2 + 10 * BATCH))
            for c in range(CHUNKS):
                if c >= 4:
                    pe.wait_ge(kept, c + 1)
                nc.tensor.matmul(p[:, c % 4, :], flat[:, :], whole[:, c * ROWS:(c + 1) * ROWS, :], start=True, stop=True).then_inc(product, 1)
            pe.wait_ge(cut, 1)
            for r in range(bands):
                c = CHUNKS + r
                pe.wait_ge(kept, c + 1)
                for k in range(9):
                    y0, x0 = r * BAND + k // 3, k % 3
                    last = nc.tensor.matmul(p[:, c % 4, 0:BAND * INNER], taps[:, k, :], window[:, y0:y0 + BAND, x0:x0 + INNER], start=k == 0, stop=k == 8)
                last.then_inc(product, 1)

        @block.scalar
        def _(act):
            act.sem_inc(kept, 4)
            act.wait_ge(w_in, 16 * (2 + 10 * BATCH))
            for c in range(total):
                act.wait_ge(product, c + 1)
                if c < CHUNKS:
                    dst, src, b = out[:, c * ROWS:(c + 1) * ROWS, :], p[:, c % 4, :].rearrange("i (h w) -> i h w", w=SIDE), bias[:, 0:1]
                else:
                    if c == CHUNKS:
                        act.wait_ge(kept, CHUNKS + 4)
                    y0 = EDGE + (c - CHUNKS) * BAND
                    dst = out[:, y0:y0 + BAND, EDGE:EDGE + INNER]
                    src, b = p[:, c % 4, 0:BAND * INNER].rearrange("i (h w) -> i h w", w=INNER), bias[:, 1:2]
                nc.scalar.activation(dst, src, ACT.Identity, bias=b).then_inc(kept, 1)


def polar_mix(nc, tag, mag, ang, mag_w, mag_b, ang_w, ang_b, out_re, out_im, cols):
    steps = mag.shape[1] // cols // 2
    TWO_PI_HI, MAGIC = 6.28125, 1.5 * 2.0 ** 23
    TWO_PI_LO = 2 * math.pi - TWO_PI_HI
    with ExitStack() as ctx:
        s = Scope(nc, ctx, tag)
        w = s.sb("w", [IMAGES, 2, 128])
        bias = s.sb("bias", [IMAGES, 3])
        xb = s.sb("xb", [IMAGES, 2, 2, cols])
        big_mag = s.sb("big_mag", [IMAGES, cols])
        turn = s.sb("turn", [IMAGES, 2, cols])
        whole = s.sb("whole", [IMAGES, 2, cols])
        wave = s.sb("wave", [IMAGES, 2, cols])
        out = s.sb("out", [IMAGES, 2, 2, cols])
        p = s.ps("p", [128, 2, 2, T])
        zeroed, w_in, bias_ready = s.sem("zeroed"), s.sem("w_in"), s.sem("bias_ready")
        loaded, stored = [s.sem("loaded0"), s.sem("loaded1")], [s.sem("stored0"), s.sem("stored1")]
        product, angles, chain, reduced, waved, made = (s.sem(n) for n in ("product", "angles", "chain", "reduced", "waved", "made"))
        LINKS = 4
        v = [x.rearrange("i (k c) -> k i c", c=cols) for x in (mag, ang, out_re, out_im)]
        block = ctx.enter_context(nc.Block())

        @block.sync
        def _(sp):
            sp.wait_ge(zeroed, 1)
            load_kron(sp, w[:, 0, :], mag_w, w_in)
            load_kron(sp, w[:, 1, :], ang_w, w_in)
            for k, b_dram in enumerate((mag_b, ang_b)):
                sp.dma_start(bias[:, k:k + 1], b_dram).then_inc(w_in, 16)

            def load(n, u):
                sp.wait_ge(product, n + 1)
                for k in range(2):
                    sp.dma_start(xb[:, u, k, :], row(v[k], n)).then_inc(loaded[u], 16)

            def store(n, u):
                sp.wait_ge(made, n + 3)
                for k in range(2):
                    sp.dma_start(row(v[2 + k], n), out[:, u, k, :]).then_inc(stored[u], 16)

            for u in range(2):
                sp.sem_inc(stored[u], 32)
                load(u, u)
            with sp.Fori(0, steps - 1) as i:
                for u in range(2):
                    store(i * 2 + u, u)
                    load(i * 2 + u + 2, u)
            for u in range(2):
                store(2 * steps - 2 + u, u)
            for u in range(2):
                sp.wait_ge(stored[u], 32 * (steps + 1))

        @block.tensor
        def _(pe):
            pe.sem_inc(product, 2)
            pe.wait_ge(w_in, 16 * (2 * BATCH + 2))
            with pe.Fori(0, steps) as i:
                for u in range(2):
                    pe.wait_ge(loaded[u], i * 32 + 32)
                    pe.wait_ge(made, i * 2 + u + 1)
                    pe.wait_ge(angles, (i * 2 + u) * 2 + 1)
                    for k in range(2):
                        last = nc.tensor.matmul(p[:, u, k, 0:cols], w[:, k, :], xb[:, u, k, :], start=True, stop=True)
                    last.then_inc(product, 1)

        @block.scalar
        def _(act):
            act.sem_inc(angles, 4)
            act.wait_ge(bias_ready, 1)
            with act.Fori(0, steps) as i:
                for u in range(2):
                    n = i * 2 + u
                    act.wait_ge(product, n + 3)
                    act.wait_ge(reduced, n + 1)
                    for k in range(2):
                        nc.scalar.activation(turn[:, k, :], p[0:IMAGES, u, 1, 0:cols], ACT.Identity, bias=bias[:, 1 + k:2 + k]).then_inc(angles, 1)
                    act.wait_ge(reduced, n + 2)
                    act.wait_ge(made, n + 2)
                    nc.scalar.activation(wave[:, :, :], whole[:, :, :], ACT.Sin).then_inc(waved, 1)

        @block.vector
        def _(dve):
            dve.sem_inc(made, 2)
            dve.sem_inc(reduced, 1)
            nc.vector.memset(w[:, :, :], 0.0).then_inc(zeroed, 1)
            dve.wait_ge(w_in, 16 * (2 * BATCH + 2))
            nc.vector.tensor_scalar(bias[:, 2:3], bias[:, 1:2], math.pi / 2, None, ALU.add).then_inc(bias_ready, 1)
            with dve.Fori(0, steps) as i:
                for u in range(2):
                    n = i * 2 + u
                    done = [0]

                    def link(ins):
                        done[0] += 1
                        ins.then_inc(chain, 1)
                        dve.wait_ge(chain, n * LINKS + done[0])

                    dve.wait_ge(angles, n * 2 + 6)
                    link(nc.vector.tensor_scalar(whole[:, :, :], turn[:, :, :], 1 / (2 * math.pi), MAGIC, ALU.mult, ALU.add))
                    link(nc.vector.tensor_scalar(whole[:, :, :], whole[:, :, :], -MAGIC, None, ALU.add))
                    link(nc.vector.scalar_tensor_tensor(out=turn[:, :, :], in0=whole[:, :, :], scalar=-TWO_PI_HI, in1=turn[:, :, :], op0=ALU.mult, op1=ALU.add))
                    link(nc.vector.scalar_tensor_tensor(out=turn[:, :, :], in0=whole[:, :, :], scalar=-TWO_PI_LO, in1=turn[:, :, :], op0=ALU.mult, op1=ALU.add))
                    nc.vector.tensor_scalar(whole[:, :, :], turn[:, :, :], -math.pi, math.pi, ALU.max, ALU.min).then_inc(reduced, 1)
                    dve.wait_ge(waved, n + 1)
                    dve.wait_ge(product, n + 3)
                    dve.wait_ge(stored[u], i * 32 + 32)
                    for k in range(2):
                        last = nc.vector.scalar_tensor_tensor(out=out[:, u, k, :], in0=p[0:IMAGES, u, 0, 0:cols], scalar=bias[:, 0:1], in1=wave[:, 1 - k, :], op0=ALU.add, op1=ALU.mult)
                    last.then_inc(made, 1)


def conv_out(nc, x, x1, spectral, real, w0t, b0, w2t, out):
    F = 2 * T
    steps = HW // F // 2
    with ExitStack() as ctx:
        s = Scope(nc, ctx, "co")
        w0 = s.sb("w0", [CB, 64])
        bias = s.sb("bias", [CB, 1])
        w2 = s.sb("w2", [MID, CH])
        x0 = s.sb("x0", [CB, 2, F])
        cat = s.sb("cat", [MID, 2, F])
        xb = s.sb("xb", [CP, 2, CT, F])
        ob = s.sb("ob", [CP, 2, CT, F])
        p0 = s.ps("p0", [64, F])
        p2 = s.ps("p2", [CP, CT, F])
        w_in, zeroed = s.sem("w_in"), s.sem("zeroed")
        loaded, stored = [s.sem("loaded0"), s.sem("loaded1")], [s.sem("stored0"), s.sem("stored1")]
        small, kept, large, added = s.sem("small"), s.sem("kept"), s.sem("large"), s.sem("added")
        v = {n: a.rearrange("c b (k f) -> b k c f", f=F) for n, a in (("x1", x1), ("sp", spectral), ("re", real))}
        x_v = x.rearrange("b (t c) (k f) -> b k c t f", c=CP, f=F)
        o_v = out.rearrange("b (t c) (k f) -> b k c t f", c=CP, f=F)
        block = ctx.enter_context(nc.Block())

        @block.sync
        def _(sp):
            sp.wait_ge(zeroed, 1)
            sp.dma_start(w0[:, 0:CB], w0t).then_inc(w_in, 16)
            sp.dma_start(bias[:, :], b0).then_inc(w_in, 16)
            sp.dma_start(w2[:, :], w2t).then_inc(w_in, 16)
            for b in range(BATCH):
                with sp.Fori(0, steps) as i:
                    for u in range(2):
                        n = (b * steps + i) * 2 + u
                        k = i * 2 + u
                        sp.wait_ge(large, n + 1)
                        sp.wait_ge(added, n + 1)
                        sp.dma_start(x0[:, u, :], row(v["x1"][b], k)[0:CB]).then_inc(loaded[u], 16)
                        sp.dma_start(cat[CB:2 * CB, u, :], row(v["sp"][b], k)).then_inc(loaded[u], 16)
                        sp.dma_start(cat[2 * CB:3 * CB, u, :], row(v["re"][b], k)).then_inc(loaded[u], 16)
                        sp.dma_start(xb[:, u], row(x_v[b], k)).then_inc(loaded[u], 16)

        @block.tensor
        def _(pe):
            pe.sem_inc(large, 2)
            pe.sem_inc(small, 1)
            pe.wait_ge(w_in, 48)
            for b in range(BATCH):
                with pe.Fori(0, steps) as i:
                    for u in range(2):
                        n = (b * steps + i) * 2 + u
                        pe.wait_ge(loaded[u], (b * steps + i) * 64 + 64)
                        pe.wait_ge(kept, n + 1)
                        for half in range(2):
                            cols = slice(half * T, (half + 1) * T)
                            last = nc.tensor.matmul(p0[:, cols], w0[:, :], x0[:, u, cols], start=True, stop=True)
                        last.then_inc(small, 1)
                        pe.wait_ge(kept, n + 2)
                        pe.wait_ge(added, n + 2)
                        for t in range(CT):
                            for half in range(2):
                                cols = slice(half * T, (half + 1) * T)
                                last = nc.tensor.matmul(p2[:, t, cols], w2[:, t * CP:(t + 1) * CP], cat[:, u, cols], start=True, stop=True)
                        last.then_inc(large, 1)

        @block.scalar
        def _(act):
            act.sem_inc(kept, 1)
            for u in range(2):
                act.sem_inc(stored[u], 16)
            act.wait_ge(w_in, 48)
            for b in range(BATCH):
                with act.Fori(0, steps) as i:
                    for u in range(2):
                        n = (b * steps + i) * 2 + u
                        act.wait_ge(small, n + 2)
                        act.wait_ge(large, n + 1)
                        nc.scalar.activation(cat[0:CB, u, :], p0[0:CB, :], ACT.Identity, bias=bias[:, 0:1]).then_inc(kept, 1)
                        act.wait_ge(added, n + 3)
                        act.dma_start(row(o_v[b], i * 2 + u), ob[:, u]).then_inc(stored[u], 16)
            for u in range(2):
                act.wait_ge(stored[u], 16 * (BATCH * steps + 1))

        @block.vector
        def _(dve):
            dve.sem_inc(added, 2)
            nc.vector.memset(w0[:, :], 0.0).then_inc(zeroed, 1)
            for b in range(BATCH):
                with dve.Fori(0, steps) as i:
                    for u in range(2):
                        n = (b * steps + i) * 2 + u
                        dve.wait_ge(large, n + 3)
                        dve.wait_ge(loaded[u], (b * steps + i) * 64 + 64)
                        dve.wait_ge(stored[u], (b * steps + i) * 16 + 16)
                        nc.vector.tensor_tensor(ob[:, u], p2[:, :, :], xb[:, u], ALU.add).then_inc(added, 1)


def layer1_weights(nc, w, scale, shift, mean_of, made):
    HID = 2 * DI
    MH = HID // 128
    with ExitStack() as ctx:
        s = Scope(nc, ctx, "lw")
        w_in_t = s.sb("w_in_t", [CP, CT, HID])
        w_sc = s.sb("w_sc", [CP, BATCH, CT, HID])
        b_in_t = s.sb("b_in_t", [128, MH])
        b_sc = s.sb("b_sc", [128, BATCH, MH])
        w_out_t = s.sb("w_out_t", [128, NJ, CH])
        w_out_sc = s.sb("w_out_sc", [128, BATCH, NJ, CH])
        pw_t = s.sb("pw_t", [CP, CT, CH])
        pw_sc = s.sb("pw_sc", [CP, BATCH, CT, CH])
        b_out_t = s.sb("b_out_t", [CP, 2, CT])
        o_bias = s.sb("o_bias", [CP, BATCH, CT])
        r_w_t = s.sb("r_w_t", [CP, CT, 2])
        r_b_t = s.sb("r_b_t", [128, 2])
        means = s.sb("means", [CP, BATCH, CT, 128])
        logit = s.sb("logit", [128, BATCH, 2])
        top = s.sb("top", [128, BATCH])
        share = s.sb("share", [128, BATCH, 2])
        bn = s.sb("bn", [CP, 4, CT])
        bn_out = s.sb("bn_out", [CP, 2, CT])
        dw_b_t = s.sb("dw_b_t", [CP, CT])
        eps = s.sb("eps", [CP, 1])
        zero = s.sb("zero", [CP, CT, SIDE])
        b_ps = s.ps("b_ps", [128, MH, BATCH])
        l_ps = s.ps("l_ps", [128, BATCH, 2])
        loaded, chain, biases, logits, spread, exps, rooted, stored = (
            s.sem(n) for n in ("loaded", "chain", "biases", "logits", "spread", "exps", "rooted", "stored"))
        shift_v = shift[:, :].rearrange("c (b t) -> c t b", t=CT)
        loads = [
            (w_in_t[:, :, :], w["W_in"].rearrange("(t c) d -> c t d", c=CP)),
            (b_in_t[:, :], w["b_in"]),
            (w_out_t[:, :, :], w["W_out"].rearrange("(j p) c -> p j c", p=128)),
            (pw_t[:, :, :], w["pw_t"].rearrange("(t c) o -> c t o", c=CP)),
            (b_out_t[:, 0, :], w["b_out"]),
            (b_out_t[:, 1, :], w["pw_b"]),
            (r_w_t[:, :, :], w["r_w_t"].rearrange("(t c) o -> c t o", c=CP)),
            (r_b_t[:, :], w["r_b"].partition_broadcast(128)),
            (dw_b_t[:, :], w["dw_b"]),
        ] + [(bn[:, k, :], w[n]) for k, n in enumerate(("bn_g", "bn_b", "bn_mean", "bn_var"))]
        block = ctx.enter_context(nc.Block())

        @block.sync
        def _(sp):
            for dst, src in loads:
                sp.dma_start(dst, src).then_inc(loaded, 16)
            sp.wait_ge(chain, FINAL)
            for b in range(BATCH):
                sp.dma_start(made["w_in"][b], w_sc[:, b]).then_inc(stored, 16)
                sp.dma_start(made["b_in"][b], b_sc[:, b, :]).then_inc(stored, 16)
                sp.dma_start(made["w_out"][b], w_out_sc[:, b]).then_inc(stored, 16)
                sp.dma_start(made["pw"][b], pw_sc[:, b]).then_inc(stored, 16)
                sp.dma_start(made["b_out"][b], o_bias[:, b, :]).then_inc(stored, 16)
            sp.dma_start(made["bn"], bn_out[:, :, :]).then_inc(stored, 16)
            sp.wait_ge(stored, 16 * (5 * BATCH + 1))

        @block.tensor
        def _(pe):
            pe.wait_ge(loaded, 16 * len(loads))
            for m in range(MH):
                for t in range(CT):
                    last = nc.tensor.matmul(b_ps[:, m, :], w_in_t[:, t, m * 128:(m + 1) * 128], shift_v[:, t, :], start=t == 0, stop=t == CT - 1)
            last.then_inc(biases, 1)
            pe.wait_ge(spread, BATCH * CT)
            for b in range(BATCH):
                for t in range(CT):
                    last = nc.tensor.matmul(l_ps[:, b, :], means[:, b, t, :], r_w_t[:, t, :], start=t == 0, stop=t == CT - 1)
            last.then_inc(logits, 1)

        @block.scalar
        def _(act):
            act.wait_ge(chain, LOGITS)
            nc.scalar.activation(share[:, :, :], logit[:, :, :], ACT.Exp).then_inc(exps, 1)
            nc.scalar.activation(bn[:, 3, :], bn[:, 3, :], ACT.Sqrt, bias=eps[:, 0:1]).then_inc(rooted, 1)

        @block.vector
        def _(dve):
            done = [0]

            def link(ins):
                done[0] += 1
                ins.then_inc(chain, 1)
                dve.wait_ge(chain, done[0])

            TS, TT, STT = nc.vector.tensor_scalar, nc.vector.tensor_tensor, nc.vector.scalar_tensor_tensor
            link(nc.vector.memset(eps[:, :], EPS))
            link(nc.vector.memset(means[:, :, :, :], 0.0))
            dve.wait_ge(loaded, 16 * len(loads))
            for b in range(BATCH):
                for t in range(CT):
                    n = b * CT + t
                    TS(means[:, b, t, :], means[:, b, t, :], mean_of[:, n:n + 1], None, ALU.add).then_inc(spread, 1)
                    link(TS(w_sc[:, b, t, :], w_in_t[:, t, :], scale[:, n:n + 1], None, ALU.mult))
            dve.wait_ge(biases, 1)
            link(TT(b_sc[:, :, :], b_ps[:, :, :].rearrange("p m b -> p b m"), b_in_t[:, :].unsqueeze(1).broadcast_to([128, BATCH, MH]), ALU.add))
            dve.wait_ge(logits, 1)
            link(TT(logit[:, :, :], l_ps[:, :, :], r_b_t[:, :].unsqueeze(1).broadcast_to([128, BATCH, 2]), ALU.add))
            link(TT(top[:, :], logit[:, :, 0], logit[:, :, 1], ALU.max))
            link(TT(logit[:, :, :], logit[:, :, :], top[:, :].unsqueeze(2).broadcast_to([128, BATCH, 2]), ALU.subtract))
            assert done[0] == LOGITS
            dve.wait_ge(exps, 1)
            link(TT(top[:, :], share[:, :, 0], share[:, :, 1], ALU.add))
            link(nc.vector.reciprocal(top[:, :], top[:, :]))
            link(TT(share[:, :, :], share[:, :, :], top[:, :].unsqueeze(2).broadcast_to([128, BATCH, 2]), ALU.mult))
            for b in range(BATCH):
                link(TS(w_out_sc[:, b], w_out_t[:, :, :], share[:, b, 0:1], None, ALU.mult))
                link(TS(pw_sc[:, b], pw_t[:, :, :], share[0:CP, b, 1:2], None, ALU.mult))
                link(TS(o_bias[:, b, :], b_out_t[:, 0, :], share[0:CP, b, 0:1], None, ALU.mult))
                link(STT(out=o_bias[:, b, :], in0=b_out_t[:, 1, :], scalar=share[0:CP, b, 1:2], in1=o_bias[:, b, :], op0=ALU.mult, op1=ALU.add))
            dve.wait_ge(rooted, 1)
            link(nc.vector.reciprocal(bn[:, 3, :], bn[:, 3, :]))
            link(TT(bn_out[:, 0, :], bn[:, 0, :], bn[:, 3, :], ALU.mult))
            link(TT(bn_out[:, 1, :], dw_b_t[:, :], bn[:, 2, :], ALU.subtract))
            link(TT(bn_out[:, 1, :], bn_out[:, 1, :], bn_out[:, 0, :], ALU.mult))
            link(TT(bn_out[:, 1, :], bn_out[:, 1, :], bn[:, 1, :], ALU.add))
            assert done[0] == FINAL


LOGITS = 2 + BATCH * CT + 4
FINAL = LOGITS + 3 + 4 * BATCH + 5


def scan_input(nc, x, made, conv_w, conv_b, ident, xcs):
    PE_TAPS = 7
    DVE_TAPS = TAPS * TAPS - PE_TAPS
    XF = 2 * T
    OUT = 4
    with ExitStack() as ctx:
        s = Scope(nc, ctx, "si")
        idn = s.sb("idn", [128, 128])
        w = s.sb("w", [CP, CT, 128])
        bias = s.sb("bias", [128, 2])
        cw = s.sb("cw", [128, TAPS * TAPS])
        diag = s.sb("diag", [128, PE_TAPS, 128])
        xb = s.sb("xb", [CP, 2, CT, XF])
        plane = s.sb("plane", [128, PLANE, PLANE])
        acc = s.sb("acc", [128, 4, ROWS, SIDE])
        xc = s.sb("xc", [128, SIDE, SIDE])
        blank = s.sb("blank", [128, NJ, T])
        turned = s.sb("turned", [128, 2, OUT, T])
        p_in = s.ps("p_in", [128, 4, T])
        p_cv = s.ps("p_cv", [128, 4, T])
        id_in, w_in, diagonals, zeroed = s.sem("id_in"), s.sem("w_in"), s.sem("diagonals"), s.sem("zeroed")
        loaded = [s.sem("loaded0"), s.sem("loaded1")]
        projected, padded, convolved, tapped, activated, turns = (s.sem(n) for n in ("projected", "padded", "convolved", "tapped", "activated", "turns"))
        blank_out = s.sem("blank_out")
        plain_out, turned_out = s.sem("plain_out"), [s.sem("turned_out0"), s.sem("turned_out1")]
        PLANES = BATCH * NJ
        LOADS = HW // XF
        STORES = CHUNKS // OUT
        AHEAD = 3
        x_v = x.rearrange("b (t c) f -> b c t f", c=CP)
        block = ctx.enter_context(nc.Block())

        def chunk_view(lay, b, j, k):
            some = xcs[bass.ds(b * CHUNKS + (lay * SLOTS + 1 + k * OUT), OUT)]
            return some[:, :, bass.ds(j, 1), :].rearrange("k p o t -> p k (o t)")

        def planes(eng):
            with eng.Fori(0, BATCH) as b:
                with eng.Fori(0, NJ) as j:
                    yield b, j, b * NJ + j

        @block.sync
        def _(sp):
            sp.dma_start(idn[:, :], ident).then_inc(id_in, 16)
            sp.wait_ge(zeroed, 2)
            for n in (0, SEQ + 1, SLOTS, SLOTS + SEQ + 1):
                sp.dma_start(xcs[n], blank[:, :, :]).then_inc(blank_out, 16)
            for u in range(2):
                sp.sem_inc(turned_out[u], 16)
            for b, j, q in planes(sp):
                sp.wait_ge(activated, q * CHUNKS + 4)
                sp.dma_start(w[:, :, :], row(made["w_in_j"], b)[:, :, bass.ds(j, 1), :].rearrange("c t o m -> c t (o m)")).then_inc(w_in, 16)
                sp.dma_start(bias[:, 0:1], row(made["b_in"], b)[:, bass.ds(j, 1)], allow_slow_non_contiguous=True).then_inc(w_in, 16)
                sp.dma_start(bias[:, 1:2], row(conv_b, j)).then_inc(w_in, 16)
                sp.dma_start(cw[:, :], row(conv_w, j)).then_inc(w_in, 16)
                for k in range(LOADS):
                    sp.wait_ge(projected, q * CHUNKS + 2 * k + 2)
                    sp.dma_start(xb[:, k % 2], row(x_v, b)[:, :, k * XF:(k + 1) * XF]).then_inc(loaded[k % 2], 16)
                for k in range(STORES):
                    sp.wait_ge(turns, q * CHUNKS + (k + 1) * OUT + 1)
                    sp.dma_start(chunk_view(1, b, j, k), turned[:, k % 2]).then_inc(turned_out[k % 2], 16)
            for u in range(2):
                sp.wait_ge(turned_out[u], 16 * (PLANES * STORES // 2 + 1))
            sp.wait_ge(blank_out, 64)

        @block.tensor
        def _(pe):
            pe.sem_inc(projected, 4)
            pe.sem_inc(convolved, 1)

            def project(q, c):
                if c % 2 == 0:
                    k = c // 2
                    pe.wait_ge(loaded[k % 2], q * (16 * LOADS // 2) + 16 * (k // 2 + 1))
                pe.wait_ge(padded, q * CHUNKS + c + 1)
                for t in range(CT):
                    last = nc.tensor.matmul(p_in[:, c % 4, :], w[:, t, :], xb[:, (c // 2) % 2, t, (c % 2) * T:(c % 2 + 1) * T], start=t == 0, stop=t == CT - 1)
                last.then_inc(projected, 1)

            for b, j, q in planes(pe):
                pe.wait_ge(w_in, q * 64 + 64)
                for c in range(AHEAD):
                    project(q, c)
                pe.wait_ge(diagonals, q + 2)
                for c in range(CHUNKS):
                    if c + AHEAD < CHUNKS:
                        project(q, c + AHEAD)
                    pe.wait_ge(padded, q * CHUNKS + min(c + 2, CHUNKS) + 4)
                    pe.wait_ge(tapped, (q * CHUNKS + c - c % 2) * DVE_TAPS + c % 2 + 1)
                    for k in range(PE_TAPS):
                        y0, x0 = c * ROWS + k // TAPS, k % TAPS
                        last = nc.tensor.matmul(p_cv[:, c % 4, :], diag[:, k, :], plane[:, y0:y0 + ROWS, x0:x0 + SIDE], start=k == 0, stop=k == PE_TAPS - 1)
                    last.then_inc(convolved, 1)

        @block.scalar
        def _(act):
            act.sem_inc(padded, 4)
            act.sem_inc(activated, 4)
            act.sem_inc(plain_out, 16)
            act.sem_inc(turns, 1)

            def pad(q, c):
                act.wait_ge(projected, q * CHUNKS + c + 5)
                nc.scalar.activation(plane[:, 1 + c * ROWS:1 + (c + 1) * ROWS, 1:1 + SIDE], p_in[:, c % 4, :].rearrange("p (h w) -> p h w", w=SIDE),
                                     ACT.Identity, bias=bias[:, 0:1]).then_inc(padded, 1)

            act.wait_ge(zeroed, 1)
            for b, j, q in planes(act):
                act.wait_ge(w_in, q * 64 + 64)
                for c in range(AHEAD):
                    pad(q, c)
                act.wait_ge(plain_out, q * (16 * STORES) + 16)
                act.wait_ge(turns, q * CHUNKS + 1)
                for c in range(CHUNKS):
                    if c + AHEAD < CHUNKS:
                        pad(q, c + AHEAD)
                    act.wait_ge(tapped, (q * CHUNKS + c - c % 2 + 6) * DVE_TAPS + c % 2 - 1)
                    nc.scalar.activation(xc[:, c * ROWS:(c + 1) * ROWS, :], acc[:, c % 4],
                                         ACT.Silu, bias=bias[:, 1:2]).then_inc(activated, 1)
                    if c % OUT == OUT - 1:
                        act.wait_ge(activated, q * CHUNKS + c + 5)
                        act.dma_start(chunk_view(0, b, j, c // OUT), xc[:, (c + 1 - OUT) * ROWS:(c + 1) * ROWS, :].rearrange("p (k h) w -> p k (h w)", k=OUT)).then_inc(plain_out, 16)
                act.wait_ge(activated, (q + 1) * CHUNKS + 4)
                for c in range(CHUNKS):
                    k = c // OUT
                    if c % OUT == 0:
                        act.wait_ge(turned_out[k % 2], q * (16 * STORES // 2) + 16 * (k // 2 + 1))
                    nc.scalar.copy(turned[:, k % 2, c % OUT, :].rearrange("p (w h) -> p w h", h=SIDE),
                                   xc[:, :, c * ROWS:(c + 1) * ROWS].rearrange("p h w -> p w h")).then_inc(turns, 1)
            act.wait_ge(plain_out, 16 * (PLANES * STORES + 1))

        @block.vector
        def _(dve):
            dve.sem_inc(diagonals, 1)
            dve.sem_inc(tapped, 4 * DVE_TAPS)
            nc.vector.memset(plane[:, :, :], 0.0).then_inc(zeroed, 1)
            nc.vector.memset(blank[:, :, :], 0.0).then_inc(zeroed, 1)
            dve.wait_ge(id_in, 16)
            for b, j, q in planes(dve):
                dve.wait_ge(w_in, q * 64 + 64)
                dve.wait_ge(convolved, q * CHUNKS + 1)
                for k in range(PE_TAPS):
                    last = nc.vector.tensor_scalar(diag[:, k, :], idn[:, :], cw[:, k:k + 1], None, ALU.mult)
                last.then_inc(diagonals, 1)
                for pair in range(0, CHUNKS, 2):
                    for k in range(DVE_TAPS):
                        for e in range(2):
                            c = pair + e
                            y0, x0 = c * ROWS + (PE_TAPS + k) // TAPS, (PE_TAPS + k) % TAPS
                            if k == 0:
                                dve.wait_ge(convolved, q * CHUNKS + c + 2)
                                dve.wait_ge(activated, q * CHUNKS + c + 1)
                                before = p_cv[:, c % 4, :].rearrange("p (h w) -> p h w", w=SIDE)
                            else:
                                dve.wait_ge(tapped, (q * CHUNKS + pair + 4) * DVE_TAPS + 2 * k + e - 1)
                                before = acc[:, c % 4]
                            nc.vector.scalar_tensor_tensor(out=acc[:, c % 4], in0=plane[:, y0:y0 + ROWS, x0:x0 + SIDE], scalar=cw[:, PE_TAPS + k:PE_TAPS + k + 1],
                                                           in1=before, op0=ALU.mult, op1=ALU.add).then_inc(tapped, 1)


def scan_rows(nc, xcs, w_rows, b_rows, c_rows, dtr):
    COLS = w_rows.shape[3]
    with ExitStack() as ctx:
        s = Scope(nc, ctx, "sr")
        w = s.sb("w", [128, 2, NJ, COLS])
        xb = s.sb("xb", [128, 2, NJ, T])
        rest = s.sb("rest", [32, 2, T])
        parts = s.sb("parts", [32, 2, 3, T], BF16)
        rows = s.sb("rows", [COLS, 2, T])
        blank = s.sb("blank", [3 * 2 * NSTATE, T])
        p = s.ps("p", [COLS, 4, T])
        w_in, loaded = s.sem("w_in"), [s.sem("loaded0"), s.sem("loaded1")]
        stored, zeroed, blank_out = [s.sem("stored0"), s.sem("stored1")], s.sem("zeroed"), s.sem("blank_out")
        product, split, kept = s.sem("product"), s.sem("split"), s.sem("kept")
        SPLITS = 5
        STORES = 3
        block = ctx.enter_context(nc.Block())

        @block.sync
        def _(sp):
            sp.dma_start(w[:, :, :, :], w_rows.rearrange("l p j m -> p l j m")).then_inc(w_in, 16)
            sp.wait_ge(zeroed, 1)
            for n in (0, SEQ + 1, SLOTS, SLOTS + SEQ + 1):
                sp.dma_start(c_rows[n].rearrange("s r t -> (s r) t"), blank[:, 0:T // 2].bitcast(BF16)).then_inc(blank_out, 16)
                sp.dma_start(b_rows[n], blank[0:2 * NSTATE, :]).then_inc(blank_out, 16)
                sp.dma_start(dtr[n], blank[0:2 * DT_RANK, :]).then_inc(blank_out, 16)
            for lay in range(2):
                with sp.Fori(0, SEQ // 2) as i:
                    for u in range(2):
                        sp.wait_ge(product, lay * SEQ + i * 2 + (u + 1))
                        sp.dma_start(xb[:, u], row(xcs, i * 2 + (lay * SLOTS + 1 + u))).then_inc(loaded[u], 16)
            sp.wait_ge(blank_out, 16 * 12)

        @block.tensor
        def _(pe):
            pe.sem_inc(product, 2)
            pe.wait_ge(w_in, 16)
            for lay in range(2):
                with pe.Fori(0, SEQ // 2) as i:
                    for u in range(2):
                        n = lay * SEQ + i * 2 + u
                        pe.wait_ge(loaded[u], i * 16 + (lay * (SEQ // 2) + 1) * 16)
                        pe.wait_ge(split, n * SPLITS + SPLITS)
                        pe.wait_ge(kept, n * 2 + 2)
                        for j in range(NJ):
                            last = nc.tensor.matmul(p[:, u, :], w[:, lay, j, :], xb[:, u, j, :], start=j == 0, stop=j == NJ - 1)
                        last.then_inc(product, 1)

        @block.vector
        def _(dve):
            nc.vector.memset(blank[:, :], 0.0).then_inc(zeroed, 1)
            dve.sem_inc(split, 2 * SPLITS)
            with dve.Fori(0, SEQ) as i:
                for u in range(2):
                    n = i * 2 + u
                    done = [2 * SPLITS]

                    def link(ins):
                        done[0] += 1
                        ins.then_inc(split, 1)
                        dve.wait_ge(split, n * SPLITS + done[0])

                    dve.wait_ge(product, n + 3)
                    dve.wait_ge(stored[u], i * (16 * STORES) + 16 * STORES)
                    left = rest[:, u, :]
                    link(nc.vector.tensor_copy(parts[:, u, 0, :], p[0:32, u, :]))
                    link(nc.vector.tensor_tensor(left, p[0:32, u, :], parts[:, u, 0, :], ALU.subtract))
                    link(nc.vector.tensor_copy(parts[:, u, 1, :], left))
                    link(nc.vector.tensor_tensor(left, left, parts[:, u, 1, :], ALU.subtract))
                    link(nc.vector.tensor_copy(parts[:, u, 2, :], left))

        @block.scalar
        def _(act):
            act.sem_inc(kept, 4)
            for u in range(2):
                act.sem_inc(stored[u], 16 * STORES)
            for lay in range(2):
                with act.Fori(0, SEQ // 2) as i:
                    for u in range(2):
                        n = lay * SEQ + i * 2 + u
                        act.wait_ge(product, n + 3)
                        act.wait_ge(stored[u], i * (16 * STORES) + (lay * (SEQ // 2) + 1) * (16 * STORES))
                        nc.scalar.copy(rows[32:64, u, :], p[32:64, u, :]).then_inc(kept, 1)
                        nc.scalar.copy(rows[64:COLS, u, :], p[64:COLS, u, :]).then_inc(kept, 1)
                        act.wait_ge(kept, n * 2 + 6)
                        act.wait_ge(split, (n + 1) * SPLITS + 2 * SPLITS)
                        slot = i * 2 + (lay * SLOTS + 1 + u)
                        act.dma_start(c_rows[bass.ds(slot, 1)].rearrange("o s r t -> (o r) s t"), parts[:, u]).then_inc(stored[u], 16)
                        act.dma_start(row(b_rows, slot), rows[32:64, u, :]).then_inc(stored[u], 16)
                        act.dma_start(row(dtr, slot), rows[64:COLS, u, :]).then_inc(stored[u], 16)
            for u in range(2):
                act.wait_ge(stored[u], 16 * STORES * (SEQ + 1))


def scan_phase(nc, direction, xcs, b_rows, c_rows, dtr, y_dram, a_log, dt_w, dt_bias, selectors, ident):
    rev = direction == 1
    tag = "r" if rev else "f"
    C_LAY = SEQ * NSTATE + 1
    PREP_LAY = SEQ + 1
    RING_DBU = 4
    GROUP_B = 4
    B_CREDIT = 2 * GROUP_B
    SCAN_CREDIT = NJ * RING_DBU
    Z_AT, PREPARE_AT, POLY_AT, FINISH_AT = (1, 4, 7), (4, 7, 10), (7, 10, 13), (6, 9, 12)
    EVACUATE_AT = 2
    STEPS = 5

    if rev:
        xcs, b_rows, c_rows, dtr, y_dram = (a[::-1] for a in (xcs, b_rows, c_rows, dtr, y_dram))
        a_log, dt_w, dt_bias = (a[::-1] for a in (a_log, dt_w, dt_bias))

    def slot(lay, loc):
        return lay * (SEQ + 2) + (1 + loc)

    with ExitStack() as ctx:
        s = Scope(nc, ctx, tag)
        sb, ps, sem = s.sb, s.ps, s.sem

        sel = sb("sel", [C_ROWS, NSTATE, 128], BF16)
        idn = sb("idn", [128, 128])
        a_coef = sb("a_coef", [128, NJ, NSTATE])
        w_dt = sb("w_dt", [DT_RANK, NJ * 128])
        b_dt = sb("b_dt", [128, NJ])
        b_cap = sb("b_cap", [128, NJ])
        xc_t = sb("xc_t", [128, NJ, T])
        c_t = sb("c_t", [C_ROWS, 2, T], BF16)
        dtr_t = sb("dtr_t", [DT_RANK, T])
        dt = sb("dt", [128, 2, NJ, T])
        dtu = sb("dtu", [128, 2, NJ, T])
        b_all = sb("b_all", [128, 2, GROUP_B, T])
        dbu = sb("dbu", [128, RING_DBU, NJ, T])
        h = sb("h", [128, NSTATE, NJ, T])
        prod = sb("prod", [128, 2, NJ, T])
        y_sb = sb("y_sb", [128, NJ, T])
        t_exp = sb("t_exp", [128, T])
        t_ln = sb("t_ln", [128, 2, T])
        t_z = sb("t_z", [128, 2, T])
        t_sq = sb("t_sq", [128, T])

        big = sb("big", [128, 1])

        y_ps = ps("y_ps", [128, NJ, T])
        c_ps = ps("c_ps", [128, T])
        z_ps = ps("z_ps", [128, T])
        da_ps = ps("da_ps", [128, NJ, T])

        const_in, wts_in = sem("const_in"), sem("wts_in")
        wts_ready = sem("wts_ready")
        xc_in, dtr_in = sem("xc_in"), sem("dtr_in")
        b_in, c_in = [sem("b_in0"), sem("b_in1")], [sem("c_in0"), sem("c_in1")]
        z_ready, softp, poly_ready, small_ready, dt_ready = (sem(n) for n in ("z_ready", "softp", "poly_ready", "small_ready", "dt_ready"))
        dtu_ready, dbu_ready = sem("dtu_ready"), sem("dbu_ready")
        c_ready = sem("c_ready")
        da_ready, scanned, multiplied, summed = sem("da_ready"), sem("scanned"), sem("multiplied"), sem("summed")
        y_started, y_evac, y_stored, reset = sem("y_started"), sem("y_evac"), sem("y_stored"), sem("reset")

        block = ctx.enter_context(nc.Block())

        @block.sync
        def _(sp):
            sp.dma_start(sel[:, :, :], selectors).then_inc(const_in, 16)
            sp.dma_start(idn[:, :], ident).then_inc(const_in, 16)

            def load_xc(lay, loc):
                sp.wait_ge(dtu_ready, lay * PREP_LAY + loc + 1)
                sp.dma_start(xc_t[:, :, :], xcs[bass.ds(slot(lay, loc), 1)].rearrange("o p j t -> (o p) j t")).then_inc(xc_in, 16)

            def load_dtr(lay, loc):
                sp.wait_ge(z_ready, (lay * PREP_LAY + loc) * NJ + 1)
                sp.dma_start(dtr_t[:, :], dtr[bass.ds(slot(lay, loc), 1)].rearrange("o r t -> (o r) t")).then_inc(dtr_in, 16)

            def load_c(lay, loc, parity):
                sp.wait_ge(c_ready, lay * C_LAY + loc * NSTATE + NSTATE)
                sp.dma_start(c_t[:, parity, :], row(c_rows, slot(lay, loc))).then_inc(c_in[parity], 16)

            def load_b(lay, loc, g):
                sp.wait_ge(dbu_ready, (lay * SEQ + loc) * NSTATE + (g + 1) * GROUP_B)
                src = b_rows[bass.ds(slot(lay, loc), 1), g * GROUP_B:(g + 1) * GROUP_B, :].broadcast_to([128, GROUP_B, T])
                sp.dma_start(b_all[:, g % 2], src).then_inc(b_in[g % 2], 16)

            def chunk(lay, loc, u, last=False):
                load_dtr(lay, loc + 1)
                load_b(lay, loc, 2)
                load_xc(lay, loc + 1)
                load_c(lay, loc + 1, (u + 1) % 2)
                load_b(lay, loc, 3)
                if not last:
                    load_b(lay, loc + 1, 0)
                    load_b(lay, loc + 1, 1)

            with sp.Fori(0, 2) as lay:
                sp.wait_ge(y_stored, lay * (16 * (SEQ + 1)) + 16)
                sp.dma_start(a_coef[:, :, :], a_log[bass.ds(lay, 1)].rearrange("o (j p) n -> p (o j) n", p=128)).then_inc(wts_in, 16)
                sp.dma_start(w_dt[:, :], row(dt_w, lay)).then_inc(wts_in, 16)
                sp.dma_start(b_dt[:, :], row(dt_bias, lay)).then_inc(wts_in, 16)
                load_dtr(lay, 0)
                load_xc(lay, 0)
                load_c(lay, 0, 0)
                load_b(lay, 0, 0)
                load_b(lay, 0, 1)
                with sp.Fori(0, SEQ // 2 - 1) as i:
                    for u in range(2):
                        chunk(lay, i * 2 + u, u)
                chunk(lay, SEQ - 2, 0)
                chunk(lay, SEQ - 1, 1, last=True)
            sp.wait_ge(y_stored, 16 * (2 * (SEQ + 1) + 1))

        @block.gpsimd
        def _(pool):
            pool.sem_inc(dtu_ready, 1)
            pool.sem_inc(poly_ready, 1)
            pool.sem_inc(dbu_ready, B_CREDIT)

            def make_dtu(lay, loc, parity):
                pool.wait_ge(xc_in, (lay * PREP_LAY + loc + 1) * 16)
                pool.wait_ge(dt_ready, (lay * PREP_LAY + loc + 1) * NJ + 1)
                nc.gpsimd.tensor_tensor(dtu[:, parity], dt[:, parity], xc_t[:, :, :], ALU.mult).then_inc(dtu_ready, 1)

            def make_poly(pz):
                pool.wait_ge(softp, pz * STEPS + 2 * STEPS)
                nc.gpsimd.tensor_tensor(t_sq[:, :], t_exp[:, :], t_sq[:, :], ALU.subtract).then_inc(poly_ready, 1)

            with pool.Fori(0, 2) as lay:
                for j in range(NJ):
                    make_poly(lay * (PREP_LAY * NJ) + j)
                make_dtu(lay, 0, 0)
                with pool.Fori(0, SEQ // 2) as i:
                    for u in range(2):
                        loc = i * 2 + u
                        pool.wait_ge(dtu_ready, lay * PREP_LAY + loc + 2)
                        for n in range(NSTATE):
                            g = n // GROUP_B
                            if n % GROUP_B == 0:
                                pool.wait_ge(b_in[g % 2], (lay * SEQ + loc) * (16 * NSTATE // GROUP_B // 2) + 16 * (g // 2 + 1))
                            pool.wait_ge(scanned, (lay * SEQ + loc) * (NSTATE * NJ) + (n - RING_DBU + 1) * NJ + SCAN_CREDIT)
                            nc.gpsimd.tensor_tensor(dbu[:, n % RING_DBU], dtu[:, u],
                                                    b_all[:, g % 2, n % GROUP_B, :].unsqueeze(1).broadcast_to([128, NJ, T]),
                                                    ALU.mult).then_inc(dbu_ready, 1)
                            if n in POLY_AT:
                                j = POLY_AT.index(n)
                                make_poly((lay * PREP_LAY + loc + 1) * NJ + j)
                            if n == NSTATE - 1:
                                make_dtu(lay, loc + 1, (u + 1) % 2)

        @block.scalar
        def _(act):
            nc.scalar.preload_act_table_set("natural_log_exp_and_others")
            act.sem_inc(y_stored, 16)
            act.sem_inc(softp, STEPS)

            def prepare(pz, j, step):
                if step == 0:
                    act.wait_ge(z_ready, pz + 2)
                    act.wait_ge(poly_ready, pz + 1)
                    ins = nc.scalar.activation(t_exp[:, :], z_ps[:, :], ACT.Relu, bias=b_cap[:, j:j + 1], scale=-1.0)
                elif step == 1:
                    act.wait_ge(softp, pz * STEPS + STEPS + 1)
                    ins = nc.scalar.activation(t_exp[:, :], t_exp[:, :], ACT.Exp, bias=big[:, 0:1], scale=-1.0)
                elif step == 2:
                    act.wait_ge(small_ready, pz + 1)
                    act.wait_ge(softp, pz * STEPS + STEPS + 2)
                    ins = nc.scalar.activation(t_ln[:, j % 2, :], t_exp[:, :], ACT.Ln, bias=1.0)
                elif step == 3:
                    ins = nc.scalar.activation(t_z[:, j % 2, :], z_ps[:, :], ACT.Identity, bias=b_dt[:, j:j + 1])
                else:
                    ins = nc.scalar.activation(t_sq[:, :], t_exp[:, :], ACT.Square, scale=0.5 ** 0.5)
                ins.then_inc(softp, 1)

            def decay(chunk, n, j, u):
                act.wait_ge(scanned, chunk * (NSTATE * NJ) + (n - 1) * NJ + j + 1 + SCAN_CREDIT)
                nc.scalar.activation(da_ps[:, j, :], dt[:, u, j, :], ACT.Exp, scale=a_coef[:, j, n:n + 1]).then_inc(da_ready, 1)

            def evacuate(lay, loc, j):
                if j == 0:
                    act.wait_ge(y_started, lay + 1)
                    act.wait_ge(summed, (lay * SEQ + loc) * NSTATE + 2)
                    act.wait_ge(y_stored, (lay * PREP_LAY + loc) * 16 + 16)
                nc.scalar.copy(y_sb[:, j, :], y_ps[:, j, :]).then_inc(y_evac, 1)

            def store(lay, loc):
                act.wait_ge(y_evac, (lay * PREP_LAY + loc) * NJ + NJ)
                act.dma_start(y_dram[bass.ds(slot(lay, loc - 1), 1)].rearrange("o p j t -> (o p) j t"), y_sb[:, :, :]).then_inc(y_stored, 16)

            act.wait_ge(reset, 1)
            with act.Fori(0, 2) as lay:
                act.wait_ge(wts_in, lay * 48 + 48)
                act.wait_ge(wts_ready, lay * 4 + 2)
                nc.scalar.activation(a_coef[:, :, :], a_coef[:, :, :], ACT.Exp).then_inc(wts_ready, 1)
                act.wait_ge(wts_ready, lay * 4 + 4)
                for j in range(NJ):
                    for step in range(STEPS):
                        prepare(lay * (PREP_LAY * NJ) + j, j, step)
                with act.Fori(0, SEQ // 2) as i:
                    for u in range(2):
                        loc = i * 2 + u
                        for n in range(NSTATE):
                            for j in range(NJ):
                                if n == 0:
                                    act.wait_ge(dt_ready, (lay * PREP_LAY + loc) * NJ + j + 2)
                                decay(lay * SEQ + loc, n, j, u)
                                if n == EVACUATE_AT:
                                    evacuate(lay, loc, j)
                                for k, at in enumerate(PREPARE_AT):
                                    step = (n - at) * NJ + j - 1
                                    if 0 <= step < STEPS:
                                        prepare((lay * PREP_LAY + loc + 1) * NJ + k, k, step)
                            if n == EVACUATE_AT + 1:
                                store(lay, loc)
                for j in range(NJ):
                    evacuate(lay, SEQ, j)
                store(lay, SEQ)

        @block.vector
        def _(dve):
            nc.vector.memset(big[:, :], BIG).then_inc(reset, 1)
            dve.sem_inc(dt_ready, 1)
            dve.sem_inc(small_ready, 1)
            dve.sem_inc(scanned, SCAN_CREDIT)
            dve.sem_inc(multiplied, 1)

            def finish_dt(pz, j, parity):
                small = t_ln[:, j % 2, :]
                dve.wait_ge(poly_ready, pz + 2)
                nc.vector.scalar_tensor_tensor(out=small, in0=small, scalar=-SAFE_GAP, in1=t_sq[:, :],
                                               op0=ALU.add, op1=ALU.max).then_inc(small_ready, 1)
                dve.wait_ge(small_ready, pz + 2)
                nc.vector.tensor_tensor(dt[:, parity, j, :], t_z[:, j % 2, :], small, ALU.max).then_inc(dt_ready, 1)

            edge = 0 if rev else T - 1

            def multiply(lay, loc, chunk, n):
                dve.wait_ge(c_ready, lay * C_LAY + loc * NSTATE + n + 1 + 2 * NSTATE)
                dve.wait_ge(scanned, chunk * (NSTATE * NJ) + n * NJ + NJ + SCAN_CREDIT)
                dve.wait_ge(summed, chunk * NSTATE + n + 1)
                nc.vector.tensor_tensor(prod[:, n % 2], h[:, n],
                                        c_ps[:, :].unsqueeze(1).broadcast_to([128, NJ, T]),
                                        ALU.mult).then_inc(multiplied, 1)

            with dve.Fori(0, 2) as lay:
                dve.wait_ge(wts_in, lay * 48 + 48)
                nc.vector.tensor_scalar(b_cap[:, :], b_dt[:, :], -1.0, BIG, ALU.mult, ALU.add).then_inc(wts_ready, 1)
                nc.vector.tensor_scalar(a_coef[:, :, :], a_coef[:, :, :], LOG_CAP, None, ALU.min).then_inc(wts_ready, 1)
                dve.wait_ge(wts_ready, lay * 4 + 3)
                nc.vector.tensor_scalar(a_coef[:, :, :], a_coef[:, :, :], -1.0, None, ALU.mult).then_inc(wts_ready, 1)
                for j in range(NJ):
                    finish_dt(lay * (PREP_LAY * NJ) + j, j, 0)
                with dve.Fori(0, BATCH) as b:
                    dve.wait_ge(multiplied, (lay * SEQ + b * CHUNKS) * NSTATE + 1)
                    nc.vector.memset(h[:, :, :, edge:edge + 1], 0.0).then_inc(reset, 1)
                    with dve.Fori(0, CHUNKS // 2) as i:
                        for u in range(2):
                            loc = b * CHUNKS + i * 2 + u
                            chunk = lay * SEQ + loc
                            dve.wait_ge(reset, lay * BATCH + b + 2)
                            dve.wait_ge(multiplied, chunk * NSTATE + 1)
                            for n in range(NSTATE):
                                dve.wait_ge(dbu_ready, chunk * NSTATE + n + 1 + B_CREDIT)
                                for j in range(NJ):
                                    dve.wait_ge(da_ready, chunk * (NSTATE * NJ) + n * NJ + j + 1)
                                    step = slice(None, None, -1) if rev else slice(None)
                                    nc.vector.tensor_tensor_scan(h[:, n, j, step], da_ps[:, j, step],
                                                                 dbu[:, n % RING_DBU, j, step], h[:, n, j, edge:edge + 1],
                                                                 ALU.mult, ALU.add).then_inc(scanned, 1)
                                if n:
                                    multiply(lay, loc, chunk, n - 1)
                                if n in FINISH_AT:
                                    j = FINISH_AT.index(n)
                                    finish_dt((lay * PREP_LAY + loc + 1) * NJ + j, j, (u + 1) % 2)
                            multiply(lay, loc, chunk, NSTATE - 1)

        @block.tensor
        def _(pe):
            pe.sem_inc(z_ready, 1)
            pe.sem_inc(c_ready, 2 * NSTATE)
            pe.sem_inc(summed, 2)

            def z_product(pz, j):
                pe.wait_ge(softp, pz * STEPS + STEPS - 1)
                nc.tensor.matmul(z_ps[:, :], w_dt[:, j * 128:(j + 1) * 128], dtr_t[:, :], start=True, stop=True).then_inc(z_ready, 1)

            def spread_c(n, parity):
                nc.tensor.matmul(c_ps[:, :], sel[:, n, :], c_t[:, parity, :], start=True, stop=True).then_inc(c_ready, 1)

            def sum_up(lay, loc, n):
                for j in range(NJ):
                    if n == 0:
                        pe.wait_ge(y_evac, (lay * PREP_LAY + loc) * NJ + j + 1)
                    last = nc.tensor.matmul(y_ps[:, j, :], idn[:, :], prod[:, n % 2, j, :], start=n == 0, stop=n == NSTATE - 1)
                last.then_inc(summed, 1)

            pe.wait_ge(const_in, 32)
            with pe.Fori(0, 2) as lay:
                pe.wait_ge(wts_in, lay * 48 + 48)
                pe.wait_ge(dtr_in, lay * (PREP_LAY * 16) + 16)
                for j in range(NJ):
                    z_product(lay * (PREP_LAY * NJ) + j, j)
                pe.wait_ge(c_in[0], lay * ((SEQ // 2 + 1) * 16) + 16)
                pe.wait_ge(multiplied, lay * (SEQ * NSTATE) + 1)
                spread_c(0, 0)
                pe.wait_ge(y_stored, lay * (PREP_LAY * 16) + 16)
                for j in range(NJ):
                    last = nc.tensor.matmul(y_ps[:, j, :], sel[:, 0, :], sel[:, 0:4, :], start=True, stop=True)
                last.then_inc(y_started, 1)
                with pe.Fori(0, SEQ // 2) as i:
                    for u in range(2):
                        loc = i * 2 + u
                        chunk = lay * SEQ + loc
                        for n in range(NSTATE):
                            if n == NSTATE - 1:
                                pe.wait_ge(c_in[(u + 1) % 2], lay * ((SEQ // 2 + 1 - (u + 1) % 2) * 16) + (i + 1 + u) * 16)
                            pe.wait_ge(multiplied, chunk * NSTATE + n + 2)
                            spread_c((n + 1) % NSTATE, (u + (n + 1) // NSTATE) % 2)
                            if n in Z_AT:
                                j = Z_AT.index(n)
                                if j == 0:
                                    pe.wait_ge(dtr_in, (lay * PREP_LAY + loc + 2) * 16)
                                z_product((lay * PREP_LAY + loc + 1) * NJ + j, j)
                            sum_up(lay, loc, n)


def sum_directions(nc, y_f, y_r, xcs, skip_w, total):
    GROUP_C = 4
    GROUPS = CHUNKS // GROUP_C
    COLS = GROUP_C * T
    PAIRS = BATCH // 2
    with ExitStack() as ctx:
        s = Scope(nc, ctx, "sd")
        cols_sum = s.sb("cols_sum", [128, 2, SIDE, SIDE])
        back = s.sb("back", [128, 2, COLS])
        rows_sum = s.sb("rows_sum", [128, 2, COLS])
        rows_back = s.sb("rows_back", [128, 2, COLS])
        xc = s.sb("xc", [128, 2, COLS])
        ds = s.sb("ds", [128, NJ, 4])
        ds_sum = s.sb("ds_sum", [128, NJ])
        ds_in = s.sem("ds_in")
        plane_in = [s.sem("plane_in0"), s.sem("plane_in1")]
        back_in = [s.sem("back_in0"), s.sem("back_in1")]
        rows_in = [s.sem("rows_in0"), s.sem("rows_in1")]
        stored = [s.sem("stored0"), s.sem("stored1")]
        merged, skipped, backed, summed, ds_ready = (s.sem(n) for n in ("merged", "skipped", "backed", "summed", "ds_ready"))
        CREDIT = 2 * GROUPS
        block = ctx.enter_context(nc.Block())

        def planes(eng):
            with eng.Fori(0, NJ) as j:
                with eng.Fori(0, PAIRS) as i:
                    for u in range(2):
                        yield j, i * 2 + u, j * BATCH + i * 2 + u, u, j * PAIRS + i

        def chunk_view(src, lay, b, j, first, count):
            some = src[bass.ds(b * CHUNKS + (lay * SLOTS + 1 + first), count)]
            return some[:, :, bass.ds(j, 1), :].rearrange("k p o t -> p k (o t)")

        @block.sync
        def _(sp):
            sp.dma_start(ds[:, :, :], skip_w).then_inc(ds_in, 16)
            for u in range(2):
                sp.sem_inc(stored[u], 16)
            for j, b, q, u, pair in planes(sp):
                for g in range(GROUPS + 1):
                    if g < GROUPS:
                        sp.wait_ge(stored[g % 2], q * (16 * GROUPS // 2) + 16 * (g // 2 + 1))
                        for dst, src in ((rows_sum, y_f), (rows_back, y_r), (xc, xcs)):
                            sp.dma_start(dst[:, g % 2, :].rearrange("p (k t) -> p k t", t=T),
                                         chunk_view(src, 0, b, j, g * GROUP_C, GROUP_C)).then_inc(rows_in[g % 2], 16)
                    if g:
                        k = g - 1
                        sp.wait_ge(summed, q * GROUPS + k + 1 + CREDIT)
                        dst = total[bass.ds(b * CHUNKS + k * GROUP_C, GROUP_C)][:, :, bass.ds(j, 1), :].rearrange("k p o t -> p k (o t)")
                        sp.dma_start(dst, rows_sum[:, k % 2, :].rearrange("p (k t) -> p k t", t=T)).then_inc(stored[k % 2], 16)
            for u in range(2):
                sp.wait_ge(stored[u], 16 * (NJ * BATCH * GROUPS // 2 + 1))

        @block.scalar
        def _(act):
            for j, b, q, u, pair in planes(act):
                act.wait_ge(summed, (q - 1) * GROUPS + CREDIT)
                act.dma_start(cols_sum[:, u, :, :].rearrange("p (k a) b -> p k (a b)", a=ROWS), chunk_view(y_f, 1, b, j, 0, CHUNKS)).then_inc(plane_in[u], 16)
                for g in range(GROUPS):
                    act.wait_ge(merged, q * GROUPS + g + 1)
                    act.dma_start(back[:, g % 2, :].rearrange("p (k t) -> p k t", t=T),
                                  chunk_view(y_r, 1, b, j, g * GROUP_C, GROUP_C)).then_inc(back_in[g % 2], 16)

        @block.vector
        def _(dve):
            dve.sem_inc(merged, 2)
            dve.sem_inc(summed, CREDIT)
            dve.wait_ge(ds_in, 16)
            nc.vector.tensor_reduce(ds_sum[:, :], ds[:, :, :], mybir.AxisListType.X, ALU.add).then_inc(ds_ready, 1)
            dve.wait_ge(ds_ready, 1)
            for j, b, q, u, pair in planes(dve):
                dve.wait_ge(plane_in[u], pair * 16 + 16)
                for g in range(GROUPS):
                    dve.wait_ge(back_in[g % 2], q * (16 * GROUPS // 2) + 16 * (g // 2 + 1))
                    part = cols_sum[:, u, g * GROUP_C * ROWS:(g + 1) * GROUP_C * ROWS, :].rearrange("p a b -> p (a b)")
                    nc.vector.tensor_tensor(part, part, back[:, g % 2, :], ALU.add).then_inc(merged, 1)
                dve.wait_ge(merged, (q + 1) * GROUPS + 2)
                for g in range(GROUPS):
                    dve.wait_ge(rows_in[g % 2], q * (48 * GROUPS // 2) + 48 * (g // 2 + 1))
                    acc = rows_sum[:, g % 2, :]
                    acc_v = acc.rearrange("p (h w) -> p h w", w=SIDE)
                    turned = cols_sum[:, u, :, g * GROUP_C * ROWS:(g + 1) * GROUP_C * ROWS].rearrange("p w h -> p h w")
                    nc.vector.scalar_tensor_tensor(out=acc, in0=xc[:, g % 2, :], scalar=ds_sum[:, bass.ds(j, 1)], in1=acc, op0=ALU.mult, op1=ALU.add).then_inc(skipped, 1)
                    dve.wait_ge(skipped, q * GROUPS + g + 1)
                    nc.vector.tensor_tensor(acc, acc, rows_back[:, g % 2, :], ALU.add).then_inc(backed, 1)
                    dve.wait_ge(backed, q * GROUPS + g + 1)
                    nc.vector.tensor_tensor(acc_v, acc_v, turned, ALU.add).then_inc(summed, 1)


def gated_output(nc, x, total, made, scale, shift, ln_g, ln_b, dw_w, out):
    K3 = 3
    HALO = ROWS + 2
    with ExitStack() as ctx:
        s = Scope(nc, ctx, "go")
        w_z = s.sb("w_z", [CP, CT, DI])
        b_z = s.sb("b_z", [128, NJ])
        w_o = s.sb("w_o", [128, NJ, CH])
        pw = s.sb("pw", [CP, CT, CH])
        b_o = s.sb("b_o", [CP, CT])
        norm = s.sb("norm", [CP, 2, CT])
        bn = s.sb("bn", [CP, 2, CT])
        lg = s.sb("lg", [128, NJ])
        lb = s.sb("lb", [128, NJ])
        cw = s.sb("cw", [CP, CT, K3 * K3])
        ones = s.sb("ones", [128, 128])
        eps = s.sb("eps", [128, 1])
        xr = s.sb("xr", [CP, 2, CT, HALO * SIDE])
        xn = s.sb("xn", [CP, 2, CT, HALO, SIDE + 2])
        y = s.sb("y", [128, 2, NJ, T])
        silu = s.sb("silu", [128, 2, NJ, T])
        sq = s.sb("sq", [128, NJ, T])
        log_var = s.sb("log_var", [128, T])
        rstd = s.sb("rstd", [128, T])
        gate = s.sb("gate", [128, 2, NJ, T])
        conv = s.sb("conv", [CP, CT, ROWS, SIDE])
        local = s.sb("local", [CP, 2, CT, T])
        result = s.sb("result", [CP, 2, CT, T])
        z_ps = s.ps("z_ps", [128, NJ, T])
        mean_ps = s.ps("mean_ps", [128, T])
        var_ps = s.ps("var_ps", [128, T])
        o_ps = s.ps("o_ps", [CP, CT, T])
        const_in, weights_in, zeroed = s.sem("const_in"), s.sem("weights_in"), s.sem("zeroed")
        x_in, y_in, stored = ([s.sem(f"{n}{u}") for u in range(2)] for n in ("x_in", "y_in", "stored"))
        mean_ready, z_ready, var_ready, o_ready = (s.sem(n) for n in ("mean_ready", "z_ready", "var_ready", "o_ready"))
        centred, squared, logged, recip, normed, scaled, gated = (s.sem(n) for n in ("centred", "squared", "logged", "recip", "normed", "scaled", "gated"))
        silus, padded, edged, taps, locals_, held, finished = (s.sem(n) for n in ("silus", "padded", "edged", "taps", "locals", "held", "finished"))
        N_TAPS = CT * K3 * K3
        N_WEIGHTS = 7
        MIDDLE = slice(SIDE, SIDE + T)
        PER_BUF = 16 * CHUNKS // 2
        x_v = x.rearrange("b (t c) f -> b c t f", c=CP)
        o_v = out.rearrange("b (t c) f -> b c t f", c=CP)
        tiles = (CHUNKS - 2) // 2
        consts = [(lg[:, :], ln_g), (lb[:, :], ln_b), (cw[:, :, :], dw_w), (bn[:, :, :], made["bn"])]
        block = ctx.enter_context(nc.Block())

        def inside(b, i, u):
            return b, i * 2 + u, i + u // 2, u % 2

        def number(c):
            return c[0] * CHUNKS + c[1]

        def due(c, credit=0):
            return c[0] * PER_BUF + c[2] * 16 + (16 + credit)

        def plain(b, chunk):
            return b, chunk, chunk // 2, chunk % 2

        @block.sync
        def _(sp):
            for dst, src in consts:
                sp.dma_start(dst, src).then_inc(const_in, 16)
            for u in range(2):
                sp.sem_inc(stored[u], 16)

            def load(c, first=False, last=False):
                n, u = number(c), c[3]
                sp.wait_ge(z_ready, n + 1)
                sp.wait_ge(padded, n + 1)
                sp.wait_ge(held, n + 1)
                r0, r1 = (1 if first else 0), (HALO - 1 if last else HALO)
                sp.dma_start(xr[:, u, :, r0 * SIDE:r1 * SIDE], row(x_v, c[0])[:, :, bass.ds(c[1] * T + (r0 - 1) * SIDE, (r1 - r0) * SIDE)]).then_inc(x_in[u], 16)
                sp.wait_ge(scaled, n + 1)
                sp.dma_start(y[:, u], row(total, n)).then_inc(y_in[u], 16)

            def store(c):
                sp.wait_ge(finished, number(c) + 2)
                sp.dma_start(row(o_v, c[0])[:, :, bass.ds(c[1] * T, T)], result[:, c[3]]).then_inc(stored[c[3]], 16)

            with sp.Fori(0, BATCH) as b:
                sp.wait_ge(finished, b * CHUNKS + 1)
                for dst, src in ((w_z[:, :, :], row(made["w_in"], b)[:, :, DI:2 * DI]), (b_z[:, :], row(made["b_in"], b)[:, NJ:2 * NJ]),
                                 (w_o[:, :, :], row(made["w_out"], b)), (pw[:, :, :], row(made["pw"], b)), (b_o[:, :], row(made["b_out"], b)),
                                 (norm[:, 0, :], scale[:, bass.ds(b * CT, CT)]), (norm[:, 1, :], shift[:, bass.ds(b * CT, CT)])):
                    sp.dma_start(dst, src).then_inc(weights_in, 16)
                load(plain(b, 0), first=True)
                load(plain(b, 1))
                with sp.Fori(0, tiles - 1) as i:
                    for u in range(2):
                        load(inside(b, i, u + 2))
                        store(inside(b, i, u))
                load(plain(b, CHUNKS - 2))
                store(plain(b, CHUNKS - 4))
                load(plain(b, CHUNKS - 1), last=True)
                for k in (3, 2, 1):
                    store(plain(b, CHUNKS - k))
            for u in range(2):
                sp.wait_ge(stored[u], BATCH * PER_BUF + 16)

        @block.tensor
        def _(pe):
            pe.sem_inc(z_ready, 2)
            pe.sem_inc(var_ready, 1)
            pe.sem_inc(o_ready, 2)
            pe.wait_ge(zeroed, 3)

            def head(c):
                n, u = number(c), c[3]
                pe.wait_ge(y_in[u], due(c))
                pe.wait_ge(centred, n + 1)
                for j in range(NJ):
                    last = nc.tensor.matmul(mean_ps[:, :], ones[:, :], y[:, u, j, :], start=j == 0, stop=j == NJ - 1)
                last.then_inc(mean_ready, 1)
                pe.wait_ge(x_in[u], due(c))
                pe.wait_ge(silus, n + 1)
                for j in range(NJ):
                    for t in range(CT):
                        last = nc.tensor.matmul(z_ps[:, j, :], w_z[:, t, j * 128:(j + 1) * 128], xr[:, u, t, MIDDLE], start=t == 0, stop=t == CT - 1)
                last.then_inc(z_ready, 1)
                pe.wait_ge(squared, n + 1)
                pe.wait_ge(logged, n + 1)
                for j in range(NJ):
                    last = nc.tensor.matmul(var_ps[:, :], ones[:, :], sq[:, j, :], start=j == 0, stop=j == NJ - 1)
                last.then_inc(var_ready, 1)

            def tail(c):
                n, u = number(c), c[3]
                pe.wait_ge(locals_, n + 2)
                pe.wait_ge(finished, n + 1)
                pe.wait_ge(gated, n + 3)
                for m in range(CT):
                    cols = slice(m * CP, (m + 1) * CP)
                    for t in range(CT):
                        nc.tensor.matmul(o_ps[:, m, :], pw[:, t, cols], local[:, u, t, :], start=t == 0, stop=False)
                    for j in range(NJ):
                        last = nc.tensor.matmul(o_ps[:, m, :], w_o[:, j, cols], gate[:, u, j, :], start=False, stop=j == NJ - 1)
                last.then_inc(o_ready, 1)

            with pe.Fori(0, BATCH) as b:
                pe.wait_ge(weights_in, b * (16 * N_WEIGHTS) + 16 * N_WEIGHTS)
                head(plain(b, 0))
                with pe.Fori(0, tiles) as i:
                    for u in range(2):
                        head(inside(b, i, u + 1))
                        tail(inside(b, i, u))
                head(plain(b, CHUNKS - 1))
                tail(plain(b, CHUNKS - 2))
                tail(plain(b, CHUNKS - 1))

        @block.scalar
        def _(act):
            act.sem_inc(silus, 1)
            act.sem_inc(recip, 1)
            act.sem_inc(padded, 2)
            act.sem_inc(held, 2)
            act.sem_inc(scaled, 2)
            act.sem_inc(logged, 1)
            act.sem_inc(locals_, 1)
            act.wait_ge(zeroed, 3)
            act.wait_ge(const_in, 16 * len(consts))

            def pad(c, first=False, last=False):
                n, u = number(c), c[3]
                r0, r1 = (1 if first else 0), (HALO - 1 if last else HALO)
                act.wait_ge(x_in[u], due(c))
                act.wait_ge(taps, n * N_TAPS + N_TAPS)
                for t in range(CT):
                    ins = nc.scalar.activation(xn[:, u, t, r0:r1, 1:1 + SIDE], xr[:, u, t, r0 * SIDE:r1 * SIDE].rearrange("p (h w) -> p h w", w=SIDE),
                                               ACT.Identity, scale=norm[:, 0, t:t + 1], bias=norm[:, 1, t:t + 1])
                ins.then_inc(padded, 1)

            def hold(c):
                u = c[3]
                act.wait_ge(stored[u], due(c))
                for t in range(CT):
                    ins = nc.scalar.activation(result[:, u, t, :], xr[:, u, t, MIDDLE], ACT.Identity, bias=b_o[:, t:t + 1])
                ins.then_inc(held, 1)

            def affine(c):
                n, u = number(c), c[3]
                act.wait_ge(o_ready, n + 1)
                act.wait_ge(normed, n + 2)
                for j in range(NJ):
                    ins = nc.scalar.activation(gate[:, u, j, :], y[:, u, j, :], ACT.Identity, scale=lg[:, j:j + 1], bias=lb[:, j:j + 1])
                ins.then_inc(scaled, 1)

            def head(c):
                n, u = number(c), c[3]
                act.wait_ge(var_ready, n + 1)
                act.wait_ge(centred, n + 2)
                nc.scalar.activation(sq[:, :, :], y[:, u], ACT.Square).then_inc(squared, 1)
                hold(c)
                act.wait_ge(z_ready, n + 3)
                act.wait_ge(gated, n + 1)
                for j in range(NJ):
                    ins = nc.scalar.activation(silu[:, u, j, :], z_ps[:, j, :], ACT.Silu, bias=b_z[:, j:j + 1])
                ins.then_inc(silus, 1)
                act.wait_ge(recip, n + 1)
                act.wait_ge(var_ready, n + 2)
                nc.scalar.activation(log_var[:, :], var_ps[:, :], ACT.Ln, bias=eps[:, 0:1]).then_inc(logged, 1)
                act.wait_ge(normed, n + 1)
                act.wait_ge(logged, n + 2)
                nc.scalar.activation(rstd[:, :], log_var[:, :], ACT.Exp, scale=-0.5).then_inc(recip, 1)
                act.wait_ge(o_ready, n + 1)
                act.wait_ge(taps, n * N_TAPS + 3 * N_TAPS)
                for t in range(CT):
                    ins = nc.scalar.activation(local[:, u, t, :], conv[:, t, :, :].rearrange("p h w -> p (h w)"), ACT.Relu, scale=bn[:, 0, t:t + 1], bias=bn[:, 1, t:t + 1])
                ins.then_inc(locals_, 1)

            with act.Fori(0, BATCH) as b:
                act.wait_ge(weights_in, b * (16 * N_WEIGHTS) + 16 * N_WEIGHTS)
                pad(plain(b, 0), first=True)
                head(plain(b, 0))
                with act.Fori(0, tiles) as i:
                    for u in range(2):
                        pad(inside(b, i, u + 1))
                        affine(inside(b, i, u))
                        head(inside(b, i, u + 1))
                pad(plain(b, CHUNKS - 1), last=True)
                affine(plain(b, CHUNKS - 2))
                head(plain(b, CHUNKS - 1))
                affine(plain(b, CHUNKS - 1))

        @block.gpsimd
        def _(pool):
            pool.sem_inc(gated, 2)
            with pool.Fori(0, SEQ // 2) as i:
                for u in range(2):
                    n = i * 2 + u
                    pool.wait_ge(scaled, n + 3)
                    pool.wait_ge(silus, n + 2)
                    nc.gpsimd.tensor_tensor(gate[:, u], gate[:, u], silu[:, u], ALU.mult).then_inc(gated, 1)

        @block.vector
        def _(dve):
            dve.sem_inc(centred, 1)
            dve.sem_inc(normed, 1)
            dve.sem_inc(taps, 2 * N_TAPS)
            dve.sem_inc(finished, 1)
            nc.vector.memset(ones[:, :], 1.0 / DI).then_inc(zeroed, 1)
            nc.vector.memset(eps[:, :], EPS).then_inc(zeroed, 1)
            nc.vector.memset(xn[:, :, :, :, :], 0.0).then_inc(zeroed, 1)
            dve.wait_ge(const_in, 16 * len(consts))
            dve.wait_ge(zeroed, 3)

            def centre(c):
                n, u = number(c), c[3]
                dve.wait_ge(mean_ready, n + 1)
                nc.vector.tensor_tensor(y[:, u], y[:, u], mean_ps[:, :].unsqueeze(1).broadcast_to([128, NJ, T]), ALU.subtract).then_inc(centred, 1)

            def edge(c, at):
                dve.wait_ge(taps, number(c) * N_TAPS + N_TAPS)
                nc.vector.memset(xn[:, c[3], :, at, :], 0.0).then_inc(edged, 1)

            def depthwise(c):
                n, u = number(c), c[3]
                dve.wait_ge(padded, n + 3)
                dve.wait_ge(locals_, n + 1)
                for k in range(K3 * K3):
                    for t in range(CT):
                        src = xn[:, u, t, k // K3:k // K3 + ROWS, k % K3:k % K3 + SIDE]
                        factor = cw[:, t, k:k + 1]
                        if k == 0:
                            nc.vector.tensor_scalar(conv[:, t], src, factor, None, ALU.mult).then_inc(taps, 1)
                        else:
                            dve.wait_ge(taps, n * N_TAPS + (2 * N_TAPS + k * CT + t - 1))
                            nc.vector.scalar_tensor_tensor(out=conv[:, t], in0=src, scalar=factor, in1=conv[:, t], op0=ALU.mult, op1=ALU.add).then_inc(taps, 1)

            def normalise(c):
                n, u = number(c), c[3]
                dve.wait_ge(recip, n + 2)
                nc.vector.tensor_tensor(y[:, u], y[:, u], rstd[:, :].unsqueeze(1).broadcast_to([128, NJ, T]), ALU.mult).then_inc(normed, 1)

            def finish(c):
                n, u = number(c), c[3]
                dve.wait_ge(held, n + 3)
                dve.wait_ge(o_ready, n + 3)
                nc.vector.tensor_tensor(result[:, u], result[:, u], o_ps[:, :, :], ALU.add).then_inc(finished, 1)

            with dve.Fori(0, BATCH) as b:
                centre(plain(b, 0))
                edge(plain(b, 0), 0)
                dve.wait_ge(edged, b * 2 + 1)
                depthwise(plain(b, 0))
                with dve.Fori(0, tiles) as i:
                    for u in range(2):
                        normalise(inside(b, i, u))
                        centre(inside(b, i, u + 1))
                        depthwise(inside(b, i, u + 1))
                        finish(inside(b, i, u))
                normalise(plain(b, CHUNKS - 2))
                centre(plain(b, CHUNKS - 1))
                edge(plain(b, CHUNKS - 1), HALO - 1)
                dve.wait_ge(edged, b * 2 + 2)
                depthwise(plain(b, CHUNKS - 1))
                finish(plain(b, CHUNKS - 2))
                normalise(plain(b, CHUNKS - 1))
                finish(plain(b, CHUNKS - 1))


TABLES = ("frft", "frft_i", "back", "back_i", "dft", "half", "half_i", "inverse", "inverse_i", "real_cos", "real_sin")
WIDTHS = (256, 256, 256, 256, 256, 2 * HALF, 2 * HALF, 256, 256, SIDE, SIDE)
AT = {name: slice(sum(WIDTHS[:k]), sum(WIDTHS[:k + 1])) for k, name in enumerate(TABLES)}


def build(nc, a, out):
    with ExitStack() as ctx:
        def dram(name, *shape, dtype=F32):
            return nc.dram_tensor(name, shape, dtype).ap()

        stats = dram("stats", BATCH * CT, CP, 2)
        x1 = dram("x1", MID, BATCH, HW)
        mag, ang, mixed = (dram(n, IMAGES, HW) for n in ("mag", "ang", "mixed"))
        re, im, spectral = (dram(n, IMAGES, HW) for n in ("re", "im", "spectral"))
        h_mag, h_ang, h_re, h_im = (dram(n, IMAGES, SIDE * HALF) for n in ("h_mag", "h_ang", "h_re", "h_im"))
        real = dram("real", IMAGES, HW)
        x_mid = dram("x_mid", BATCH, CH, HW)
        xcs, y_f, y_r = (dram(n, 2 * SLOTS, 128, NJ, T) for n in ("xcs", "y_f", "y_r"))
        b_rows, dtr = dram("b_rows", 2 * SLOTS, 2 * NSTATE, T), dram("dtr", 2 * SLOTS, 2 * DT_RANK, T)
        c_rows = dram("c_rows", 2 * SLOTS, 3, 2 * NSTATE, T, dtype=BF16)
        total = dram("total", SEQ, 128, NJ, T)
        made = dict(w_in=dram("made_w_in", BATCH, CP, CT, 2 * DI), b_in=dram("made_b_in", BATCH, 128, 2 * NJ),
                    w_out=dram("made_w_out", BATCH, 128, NJ, CH), pw=dram("made_pw", BATCH, CP, CT, CH),
                    b_out=dram("made_b_out", BATCH, CP, CT), bn=dram("made_bn", CP, 2, CT))
        made["w_in_j"] = made["w_in"].rearrange("b c t (m k) -> b c t m k", k=128)

        scale, shift, mean_of = (ctx.enter_context(nc.sbuf_tensor(n, [CP, BATCH * CT], F32)) for n in ("scale", "shift", "mean_of"))
        x = a["x"]

        def planes(array, width=SIDE):
            return array.rearrange("i (h w) -> i h w", w=width)

        def branch(k):
            return x1[k * CB:(k + 1) * CB].rearrange("c b (h w) -> (c b) h w", w=SIDE)

        channel_stats(nc, "s0", x, stats)
        norm_coefficients(nc, "n0", stats, a["group_mean"], scale, shift, mean_of)
        conv_in(nc, x, a["conv1_wt"], scale, shift, x1)
        tab = a["tables"]
        transform(nc, "ff", [branch(1)], SIDE, tab, [AT["frft"]], [AT["frft"], AT["frft_i"]], SIDE, "polar", [planes(mag), planes(ang)])
        transform(nc, "rf", [branch(2)], SIDE, tab, [AT["dft"]], [AT["half"], AT["half_i"]], HALF, "polar", [planes(h_mag, HALF), planes(h_ang, HALF)])
        inner_mix(nc, mag, a["mag_s_w"], a["mag_s_b"], a["mag_f_w"], a["mag_f_b"], mixed)
        polar_mix(nc, "pf", mixed, ang, a["mag_w"], a["mag_b"], a["pha_w"], a["pha_b"], re, im, T)
        polar_mix(nc, "pr", h_mag, h_ang, a["conv_1_w"], a["conv_1_b"], a["conv_1_w"], a["conv_1_b"], h_re, h_im, SIDE * HALF // 20)
        transform(nc, "fi", [planes(re), planes(im)], SIDE, tab, [AT["back"], AT["back_i"]], [AT["back"], AT["back_i"]], SIDE, "abs", [planes(spectral)])
        transform(nc, "ri", [planes(h_re, HALF), planes(h_im, HALF)], HALF, tab, [AT["inverse"], AT["inverse_i"]], [AT["real_cos"], AT["real_sin"]], SIDE, "real", [planes(real)])
        per_channel = [v.rearrange("(c b) f -> c b f", b=BATCH) for v in (spectral, real)]
        conv_out(nc, x, x1, per_channel[0], per_channel[1], a["conv_0_w"], a["conv_0_b"], a["conv2_wt"], x_mid)

        channel_stats(nc, "s1", x_mid, stats)
        norm_coefficients(nc, "n1", stats, a["group_mean"], scale, shift, mean_of)
        layer1_weights(nc, a, scale, shift, mean_of, made)
        scan_input(nc, x_mid, made, a["conv_w"], a["conv_b"], a["ident"], xcs)
        scan_rows(nc, xcs, a["w_rows"], b_rows, c_rows, dtr)
        for direction, y in enumerate((y_f, y_r)):
            states = slice(NSTATE * direction, NSTATE * (direction + 1))
            ranks = slice(DT_RANK * direction, DT_RANK * (direction + 1))
            scan_phase(nc, direction, xcs, b_rows[:, states], c_rows.rearrange("k s r t -> k (s r) t"), dtr[:, ranks], y,
                       a["a_log"][direction], a["dt_w"][direction], a["dt_bias"][direction], a["selectors"][direction], a["ident"])
        sum_directions(nc, y_f, y_r, xcs, a["skip_w"], total)
        gated_output(nc, x_mid, total, made, scale, shift, a["ln_g"], a["ln_b"], a["dw_w"], out)


def frft_matrix(n, order):
    before = np.eye(n, dtype=np.complex128)
    if order < 0.5:
        moved = (np.arange(n) + n // 2) % n
        before = (np.fft.ifft(before[moved, :], axis=0) * math.sqrt(n))[np.argsort(moved), :]
        order = order + 1.0
    alpha = order * math.pi / 2
    tan_half, sine = math.tan(alpha / 2), math.sin(alpha)
    c = math.pi / n / sine / 4
    m = np.arange(2 * n - 1)
    interpolate = np.sinc((m[:, None] - 2 * np.arange(n)[None]) / 2.0)
    chirp = lambda k: np.exp(-1j * math.pi / n * tan_half / 4 * k ** 2)
    q = n - 1 + 2 * np.arange(n)
    convolve = np.exp(1j * c * (q[:, None] - (m[None] + n - 1.0)) ** 2)
    after = chirp(-n + 1.0 + 2 * np.arange(n))[:, None]
    phase = np.exp(-1j * (1 - order) * math.pi / 4) * math.sqrt(c / math.pi)
    return phase * (after * (convolve @ (chirp(-n + 1.0 + m)[:, None] * interpolate))) @ before


def transform_tables():
    def pair(f):
        t = f.T
        return [np.hstack([t.real, t.imag]), np.hstack([-t.imag, t.real])]

    k = np.arange(SIDE)
    turn = np.outer(k, k) % SIDE
    cos, sin = np.cos(2 * np.pi * turn / SIDE), np.sin(2 * np.pi * turn / SIDE)
    sin[turn % (SIDE // 2) == 0] = 0
    cos[turn % (SIDE // 2) == SIDE // 4] = 0
    dft, inverse = cos - 1j * sin, (cos + 1j * sin) / SIDE
    weight = np.full(HALF, 2.0)
    weight[[0, -1]] = 1
    real_cos, real_sin = np.zeros((SIDE, SIDE)), np.zeros((SIDE, SIDE))
    real_cos[:HALF] = weight[:, None] * cos[:HALF] / SIDE
    real_sin[:HALF] = -weight[:, None] * sin[:HALF] / SIDE
    parts = pair(frft_matrix(SIDE, 0.5)) + pair(frft_matrix(SIDE, -0.5)) + pair(dft)[:1] + pair(dft[:HALF]) + pair(inverse)
    return np.hstack(parts + [real_cos, real_sin]).astype(np.float32)


def kernel(**inputs):
    import concourse.bacc as bacc
    from concourse.bass_utils import run_bass_kernel_spmd

    def l0(name):
        return np.asarray(inputs["L0_conv_" + name])

    def l1(name):
        return np.asarray(inputs["L1_conv_" + name])

    def columns(v, parts=CP):
        return v.reshape(-1, parts).T

    def per_image(v):
        return np.repeat(v, BATCH)[:, None]

    order = [(0, 1), (2, 3)]
    x_proj = l1("x_proj_w")
    w_rows = np.zeros((2, 128, NJ, 64 + 2 * DT_RANK), np.float32)
    for d in range(2):
        for lay in range(2):
            t = x_proj[order[d][lay]].T.reshape(NJ, 128, -1).transpose(1, 0, 2)
            w_rows[lay, :, :, NSTATE * d:NSTATE * (d + 1)] = t[:, :, DT_RANK + NSTATE:]
            w_rows[lay, :, :, 32 + NSTATE * d:32 + NSTATE * (d + 1)] = t[:, :, DT_RANK:DT_RANK + NSTATE]
            w_rows[lay, :, :, 64 + DT_RANK * d:64 + DT_RANK * (d + 1)] = t[:, :, :DT_RANK]
    per_dir = lambda v: np.stack([v[list(k)] for k in order])
    selectors = np.zeros((2, 3, 2, NSTATE, NSTATE, 128), np.float32)
    for d in range(2):
        selectors[d, :, d, np.arange(NSTATE), np.arange(NSTATE)] = 1
    arrays = dict(
        x=np.asarray(inputs["x"]).reshape(BATCH, CH, HW),
        group_mean=np.kron(np.eye(CP // GROUP), np.full((GROUP, GROUP), 1 / GROUP)).astype(np.float32),
        ident=np.eye(128, dtype=np.float32),
        tables=transform_tables(),
        selectors=selectors.reshape(2, C_ROWS, NSTATE, 128).astype(np.dtype("bfloat16")),
        conv1_wt=l0("conv1_w").T, conv2_wt=l0("conv2_w").T,
        mag_s_w=l0("mag_s_w").transpose(2, 3, 1, 0).reshape(9, CB, CB), mag_s_b=per_image(l0("mag_s_b")),
        mag_f_w=l0("mag_f_w").T, mag_f_b=per_image(l0("mag_f_b")),
        mag_w=l0("mag_w").T, mag_b=per_image(l0("mag_b")),
        pha_w=l0("pha_w").T, pha_b=per_image(l0("pha_b")),
        conv_0_w=l0("conv_0_w").T, conv_0_b=l0("conv_0_b")[:, None],
        conv_1_w=l0("conv_1_w").T, conv_1_b=per_image(l0("conv_1_b")),
        W_in=l1("W_in"), b_in=columns(l1("b_in"), 128), W_out=l1("W_out"), b_out=columns(l1("b_out")),
        pw_t=l1("pw_w").T, pw_b=columns(l1("pw_b")), r_w_t=l1("r_w").T, r_b=l1("r_b"),
        dw_w=l1("dw_w").reshape(CT, CP, 9).transpose(1, 0, 2), dw_b=columns(l1("dw_b")),
        bn_g=columns(l1("bn_g")), bn_b=columns(l1("bn_b")), bn_mean=columns(l1("bn_mean")), bn_var=columns(l1("bn_var")),
        ln_g=columns(l1("ln_g"), 128), ln_b=columns(l1("ln_b"), 128),
        conv_w=l1("conv_w").reshape(NJ, 128, TAPS * TAPS), conv_b=l1("conv_b").reshape(NJ, 128, 1),
        skip_w=l1("Ds").reshape(4, NJ, 128).transpose(2, 1, 0),
        w_rows=w_rows, a_log=per_dir(l1("A_log")), dt_w=per_dir(l1("dt_proj_w").transpose(0, 2, 1)),
        dt_bias=per_dir(l1("dt_proj_b").reshape(4, NJ, 128).transpose(0, 2, 1)),
    )
    arrays = {name: np.ascontiguousarray(v) for name, v in arrays.items()}
    nc = bacc.Bacc("TRN2", target_bir_lowering=False, num_devices=1)
    a = {name: nc.dram_tensor(f"in_{name}", v.shape, mybir.dt.from_np(v.dtype), kind="ExternalInput").ap() for name, v in arrays.items()}
    out = nc.dram_tensor("out", (BATCH, CH, HW), F32, kind="ExternalOutput").ap()
    build(nc, a, out)
    result = run_bass_kernel_spmd(nc, [{f"in_{name}": v for name, v in arrays.items()}], core_ids=[0])
    return result.results[0]["out"].reshape(BATCH, CH, SIDE, SIDE)
```
